# Optimizing a Trainium2 kernel written in Bass

```python
import numpy as np
import jax
import jax.numpy as jnp

def _softmax(x, axis=-1):
    return jax.nn.softmax(x, axis=axis)
def _gelu(x):
    return jax.nn.gelu(x, approximate=True)
def _silu(x):
    return jax.nn.silu(x)
def _sigmoid(x):
    return jax.nn.sigmoid(x)
def _layernorm(x, axis=-1, eps=1e-5):
    m = jnp.mean(x, axis=axis, keepdims=True)
    v = jnp.var(x, axis=axis, keepdims=True)
    return (x - m) / jnp.sqrt(v + eps)
def _scatter_add(tgt, idx, src, axis=0):
    return tgt.at[idx].add(src)
def _segment_sum(src, seg, n):
    return jax.ops.segment_sum(src, seg, n)

kernel_name = 'mk_conv_preact_d1_conv_nchw256_dfad9e'

def setup_inputs(seed: int = 0):
    np.random.seed(seed)
    _w = jnp.asarray
    def _rec_inputs():
        import jax
        import jax.numpy as jnp
        _gk = jax.random.key(seed)
        x = -0.0002091 + 1 * jax.random.normal(jax.random.fold_in(_gk, 1), (32, 256, 56, 56), jnp.float32)
        return x
    x = _rec_inputs()
    def _L0_conv_setup():
        import jax, jax.numpy as jnp
        import numpy as np
        B, C, H, W = (32, 256, 56, 56)
        HEADS, AG, GROUPS = (8, 49, 32)
        N = H * W
        HEAD_DIM = C // HEADS
        POOL = 7

        def group_norm(x, w, b, groups=GROUPS, eps=1e-05):
            Bn, Cn, Hn, Wn = x.shape
            xg = x.reshape(Bn, groups, Cn // groups, Hn, Wn)
            m = xg.mean(axis=(2, 3, 4), keepdims=True)
            v = xg.var(axis=(2, 3, 4), keepdims=True)
            xn = ((xg - m) / jnp.sqrt(v + eps)).reshape(Bn, Cn, Hn, Wn)
            return xn * w[None, :, None, None] + b[None, :, None, None]

        def conv1x1(x, w):
            return jnp.einsum('bchw,oc->bohw', x, w)
        key = jax.random.key(seed)
        ks = jax.random.split(key, 16)
        s = 0.02
        d = {}
        d['x'] = jax.random.normal(ks[0], (B, C, H, W), jnp.float32)
        for i, p in enumerate(['q', 'k', 'v', 'p']):
            d[p + '_w'] = jax.random.normal(ks[1 + i], (C, C), jnp.float32) * s
            d[p + '_gw'] = jnp.ones((C,), jnp.float32)
            d[p + '_gb'] = jnp.zeros((C,), jnp.float32)
        d['dwc_w'] = jax.random.normal(ks[5], (C, 1, 3, 3), jnp.float32) * s
        d['dwc_b'] = jnp.zeros((C,), jnp.float32)
        d['an_bias'] = jax.random.normal(ks[6], (HEADS, AG, 7, 7), jnp.float32) * s
        d['na_bias'] = jax.random.normal(ks[7], (HEADS, AG, 7, 7), jnp.float32) * s
        d['ah_bias'] = jax.random.normal(ks[8], (1, HEADS, AG, W, 1), jnp.float32) * s
        d['aw_bias'] = jax.random.normal(ks[9], (1, HEADS, AG, 1, W), jnp.float32) * s
        d['ha_bias'] = jax.random.normal(ks[10], (1, HEADS, W, 1, AG), jnp.float32) * s
        d['wa_bias'] = jax.random.normal(ks[11], (1, HEADS, 1, W, AG), jnp.float32) * s
        return d
    _L0_conv_all = _L0_conv_setup()
    _L0_conv_in = {k: v for k, v in _L0_conv_all.items() if k in ('q_w', 'q_gw', 'q_gb', 'k_w', 'k_gw', 'k_gb', 'v_w', 'v_gw', 'v_gb', 'p_w', 'p_gw', 'p_gb', 'dwc_w', 'dwc_b', 'an_bias', 'na_bias', 'ah_bias', 'aw_bias', 'ha_bias', 'wa_bias', )}
    del _L0_conv_all

    return {
        "x": x,
        "L0_conv_q_w": _L0_conv_in["q_w"],
        "L0_conv_q_gw": _L0_conv_in["q_gw"],
        "L0_conv_q_gb": _L0_conv_in["q_gb"],
        "L0_conv_k_w": _L0_conv_in["k_w"],
        "L0_conv_k_gw": _L0_conv_in["k_gw"],
        "L0_conv_k_gb": _L0_conv_in["k_gb"],
        "L0_conv_v_w": _L0_conv_in["v_w"],
        "L0_conv_v_gw": _L0_conv_in["v_gw"],
        "L0_conv_v_gb": _L0_conv_in["v_gb"],
        "L0_conv_p_w": _L0_conv_in["p_w"],
        "L0_conv_p_gw": _L0_conv_in["p_gw"],
        "L0_conv_p_gb": _L0_conv_in["p_gb"],
        "L0_conv_dwc_w": _L0_conv_in["dwc_w"],
        "L0_conv_dwc_b": _L0_conv_in["dwc_b"],
        "L0_conv_an_bias": _L0_conv_in["an_bias"],
        "L0_conv_na_bias": _L0_conv_in["na_bias"],
        "L0_conv_ah_bias": _L0_conv_in["ah_bias"],
        "L0_conv_aw_bias": _L0_conv_in["aw_bias"],
        "L0_conv_ha_bias": _L0_conv_in["ha_bias"],
        "L0_conv_wa_bias": _L0_conv_in["wa_bias"],
    }

def reference(x, L0_conv_q_w, L0_conv_q_gw, L0_conv_q_gb, L0_conv_k_w, L0_conv_k_gw, L0_conv_k_gb, L0_conv_v_w, L0_conv_v_gw, L0_conv_v_gb, L0_conv_p_w, L0_conv_p_gw, L0_conv_p_gb, L0_conv_dwc_w, L0_conv_dwc_b, L0_conv_an_bias, L0_conv_na_bias, L0_conv_ah_bias, L0_conv_aw_bias, L0_conv_ha_bias, L0_conv_wa_bias):
    import jax
    import jax.numpy as jnp
    def _L0_conv_ref(x, q_w, q_gw, q_gb, k_w, k_gw, k_gb, v_w, v_gw, v_gb, p_w, p_gw, p_gb, dwc_w, dwc_b, an_bias, na_bias, ah_bias, aw_bias, ha_bias, wa_bias):
        import jax, jax.numpy as jnp
        import numpy as np
        B, C, H, W = (32, 256, 56, 56)
        HEADS, AG, GROUPS = (8, 49, 32)
        N = H * W
        HEAD_DIM = C // HEADS
        POOL = 7

        def group_norm(x, w, b, groups=GROUPS, eps=1e-05):
            Bn, Cn, Hn, Wn = x.shape
            xg = x.reshape(Bn, groups, Cn // groups, Hn, Wn)
            m = xg.mean(axis=(2, 3, 4), keepdims=True)
            v = xg.var(axis=(2, 3, 4), keepdims=True)
            xn = ((xg - m) / jnp.sqrt(v + eps)).reshape(Bn, Cn, Hn, Wn)
            return xn * w[None, :, None, None] + b[None, :, None, None]

        def conv1x1(x, w):
            return jnp.einsum('bchw,oc->bohw', x, w)
        scale = HEAD_DIM ** (-0.5)
        q = group_norm(conv1x1(x, q_w), q_gw, q_gb)
        k = group_norm(conv1x1(x, k_w), k_gw, k_gb)
        v = group_norm(conv1x1(x, v_w), v_gw, v_gb)
        at = q.reshape(B, C, POOL, H // POOL, POOL, W // POOL).mean(axis=(3, 5))
        at = at.reshape(B, HEADS, HEAD_DIM, AG).transpose(0, 1, 3, 2)
        qh = q.reshape(B, HEADS, HEAD_DIM, N).transpose(0, 1, 3, 2)
        kh = k.reshape(B, HEADS, HEAD_DIM, N).transpose(0, 1, 3, 2)
        vh = v.reshape(B, HEADS, HEAD_DIM, N).transpose(0, 1, 3, 2)
        pb1 = jax.image.resize(an_bias, (HEADS, AG, H, W), 'bilinear').reshape(1, HEADS, AG, N)
        pb2 = (ah_bias + aw_bias).reshape(1, HEADS, AG, N)
        agent_attn = jax.nn.softmax(jnp.einsum('bhad,bhnd->bhan', at * scale, kh) + pb1 + pb2, axis=-1)
        agent_v = jnp.einsum('bhan,bhnd->bhad', agent_attn, vh)
        ab1 = jax.image.resize(na_bias, (HEADS, AG, H, W), 'bilinear').reshape(1, HEADS, AG, N).transpose(0, 1, 3, 2)
        ab2 = (ha_bias + wa_bias).reshape(1, HEADS, N, AG)
        q_attn = jax.nn.softmax(jnp.einsum('bhnd,bhad->bhna', qh * scale, at) + ab1 + ab2, axis=-1)
        xo = jnp.einsum('bhna,bhad->bhnd', q_attn, agent_v)
        xo = xo.transpose(0, 2, 1, 3).reshape(B, N, C)
        dw = jax.lax.conv_general_dilated(v, dwc_w, (1, 1), 'SAME', feature_group_count=C, dimension_numbers=('NCHW', 'OIHW', 'NCHW')) + dwc_b[None, :, None, None]
        xo = xo + dw.transpose(0, 2, 3, 1).reshape(B, N, C)
        xo = xo.transpose(0, 2, 1).reshape(B, C, H, W)
        return group_norm(conv1x1(xo, p_w), p_gw, p_gb)

    def _gn(v, G=32, eps=1e-5):
        B_, C_, H_, W_ = v.shape
        g = v.reshape(B_, G, C_ // G, H_, W_)
        m = jnp.mean(g, axis=(2, 3, 4), keepdims=True)
        s = jnp.var(g, axis=(2, 3, 4), keepdims=True)
        return ((g - m) / jnp.sqrt(s + eps)).reshape(v.shape)

    def _ln_c(v, eps=1e-6):
        m = jnp.mean(v, axis=1, keepdims=True)
        s = jnp.var(v, axis=1, keepdims=True)
        return (v - m) / jnp.sqrt(s + eps)

    def _ln_t(v, eps=1e-5):
        m = jnp.mean(v, axis=-1, keepdims=True)
        s = jnp.var(v, axis=-1, keepdims=True)
        return (v - m) / jnp.sqrt(s + eps)

    def _to_tokens(v):
        B_, C_, H_, W_ = v.shape
        return v.reshape(B_, C_, H_ * W_).transpose(0, 2, 1)
    def _from_tokens(t, like):
        B_, C_, H_, W_ = like.shape
        return t.transpose(0, 2, 1).reshape(B_, C_, H_, W_)

    x = x + _L0_conv_ref(_gn(x), L0_conv_q_w, L0_conv_q_gw, L0_conv_q_gb, L0_conv_k_w, L0_conv_k_gw, L0_conv_k_gb, L0_conv_v_w, L0_conv_v_gw, L0_conv_v_gb, L0_conv_p_w, L0_conv_p_gw, L0_conv_p_gb, L0_conv_dwc_w, L0_conv_dwc_b, L0_conv_an_bias, L0_conv_na_bias, L0_conv_ah_bias, L0_conv_aw_bias, L0_conv_ha_bias, L0_conv_wa_bias)
    return x


_drawn_inputs = setup_inputs


def setup_inputs(seed=0):
    import zlib

    import numpy as np

    out = dict(_drawn_inputs(seed))
    spreads = {'L0_conv_q_gw': (1.0, 0.6),
     'L0_conv_q_gb': (0.0, 0.1),
     'L0_conv_k_gw': (1.0, 0.6),
     'L0_conv_k_gb': (0.0, 2.0),
     'L0_conv_v_gw': (1.0, 0.2),
     'L0_conv_v_gb': (0.0, 0.1),
     'L0_conv_p_gw': (1.0, 0.2),
     'L0_conv_p_gb': (0.0, 0.1),
     'L0_conv_dwc_b': (0.0, 0.1)}
    factors = {'L0_conv_q_w': 8.0,
     'L0_conv_an_bias': 64.0,
     'L0_conv_na_bias': 64.0,
     'L0_conv_ah_bias': 64.0,
     'L0_conv_aw_bias': 64.0,
     'L0_conv_ha_bias': 64.0,
     'L0_conv_wa_bias': 64.0}
    for name, (base, spread) in spreads.items():
        noise = np.random.default_rng([zlib.crc32(name.encode()), seed]).standard_normal(out[name].shape)
        drawn = base * np.exp(spread * noise) if base else spread * noise
        out[name] = jnp.asarray(drawn.astype(out[name].dtype))
    for name, factor in factors.items():
        out[name] = (out[name] * factor).astype(out[name].dtype)
    return out
```

```python
from contextlib import ExitStack

import numpy as np

import concourse.bass as bass
from concourse import mybir

F32 = mybir.dt.float32
ALU = mybir.AluOpType
ACT = mybir.ActivationFunctionType
AX = mybir.AxisListType

P = 128
C = 256
HALVES = C // P
H = W = 56
N = H * W
HEADS = 8
HEAD_DIM = C // HEADS
AGENTS = 49
GRID = 7
CELL = H // GRID
PAIRS = HEADS // 2
PAIR = 2 * AGENTS
HALF_HEADS = HEADS // HALVES
HALF_AGENTS = HALF_HEADS * AGENTS
ALL_AGENTS = HEADS * AGENTS
GROUP = C // 32
SCALE = HEAD_DIM ** -0.5
EPS = 1e-5
RSQRT_GUESS = float(0x5F3759DF)
NEWTON = 3

ROWS = 8
CHUNK = ROWS * W
CHUNKS = H // ROWS
SUB = 112
SUBS = CHUNK // SUB
TILES = N // SUB
PATCHES = C // HEAD_DIM
BASIS_A = GRID * GRID + H
BASIS_B = W

GN_Q, GN_V, GN_K, GN_X, GN_P = range(5)
CV_PER = 2 * CHUNKS
CV_Q, CV_V, CV_K, CV_P = (j * CV_PER for j in range(4))


class Count:

    def __init__(self, sem, per, credit=0, unit=1):
        self.sem, self.per, self.credit, self.unit = sem, per, credit, unit

    def at(self, i, k):
        return i * (self.per * self.unit) + (k * self.unit + self.credit)


def attention_block(nc, B, a):
    ctx = ExitStack()
    with ctx:
        def sb(name, shape, dt=F32):
            return ctx.enter_context(nc.sbuf_tensor("sb_" + name, shape, dt))

        def sem(name):
            return ctx.enter_context(nc.semaphore(name))

        X = sb("x_norm", [P, HALVES, N])
        Q = sb("q", [P, HALVES, N])
        KP = sb("k_then_projection", [P, HALVES, N])
        V = sb("v_padded", [P, HALVES, (H + 2) * W])
        R1 = sb("scores", [P, 2, N])
        R2 = sb("transposed", [P, 2 * PAIRS * CHUNK])
        PT = sb("agent_weights_by_position", [P, 2, SUBS * PAIR])
        VG = sb("v_three_rows", [P, 2, PATCHES // 2, CHUNK])
        B1 = sb("agent_bias", [P, 4, CHUNK])
        Y = sb("attention_out", [P, 2, HALVES, CHUNK])
        XR = sb("x_again", [P, 2, HALVES, CHUNK])
        WT = sb("weights", [P, 4, HALVES, C])
        DW = sb("depthwise_diagonals", [P, PATCHES, 3, HEAD_DIM])
        CONST = sb("constants", [P, 2 * P + HEAD_DIM + 2 * HEAD_DIM])
        PAR = sb("params", [P, 5 * 2 * HALVES + HALVES])
        DWC = sb("depthwise_taps", [P, PATCHES * 3])
        M1 = sb("agents_for_k", [P, HALVES, HALF_AGENTS])
        M2 = sb("agents_for_q", [P, HALVES, HALF_AGENTS])
        AG = sb("pooled_q", [P, HALVES, AGENTS])
        AGV = sb("agent_v", [P, PAIRS, 2 * HEAD_DIM])
        AVS = sb("agent_v_channels", [P, PAIR])
        ST = sb("chunk_stats", [P, HALVES, CHUNKS, 6])
        MV = sb("channel_stats", [P, HALVES, 2])
        SQ = sb("squares", [P, HALVES])
        GS = sb("group_stats", [P, HALVES, 2])
        VAR = sb("group_variance", [P, HALVES])
        RS = sb("group_rsqrt", [P, HALVES])
        HALF_BITS = sb("halved_bits", [P, HALVES], mybir.dt.int32)
        MINUS_HALF = sb("minus_half_variance", [P, HALVES])
        AB = sb("scale_and_shift", [P, 5, 2, HALVES])
        MX = sb("chunk_maxima", [P, CHUNKS])
        MAX = sb("agent_maxima", [P, PAIRS])
        NM = sb("negative_maximum", [P, PAIRS])
        SUMS = sb("agent_sums", [P, PAIRS])
        QM = sb("query_maxima", [P, 2, SUBS * HEADS])
        QS = sb("query_sums", [P, 2, SUBS * HEADS])

        T1 = R1
        T2 = R1[:, 0, :].rearrange("p (s m) -> p s m", s=2)
        B2 = R1[:, 1, :].rearrange("p (s m) -> p s m", s=2)
        VT = R2[0:SUB, :].rearrange("p (n c) -> p n c", c=P)
        P2 = R2[:, :].rearrange("p (s g n) -> p s g n", s=2, g=PAIRS)
        V_IN = V[:, :, W:W + N]
        ident = CONST[:, 0:P]
        group_mean = CONST[:, P:2 * P]
        eye32 = CONST[:, 2 * P:2 * P + HEAD_DIM]
        pair_mask = CONST[:, 2 * P + HEAD_DIM:2 * P + 3 * HEAD_DIM]
        gn_par = PAR[:, 0:20].rearrange("p (n k t) -> p n k t", n=5, k=2)
        dwc_b = PAR[:, 20:22]

        CV = [ctx.enter_context(nc.psum_tensor(f"conv{j}", [P, 512], F32)) for j in range(2)]
        SC = [ctx.enter_context(nc.psum_tensor(f"score{j}", [P, 512], F32)) for j in range(2)]
        TR = [ctx.enter_context(nc.psum_tensor(f"turn{j}", [P, 512], F32)) for j in range(2)]
        YA = [ctx.enter_context(nc.psum_tensor(f"sum{j}", [P, 512], F32)) for j in range(2)]
        MISC = YA[1][:, 256:260]
        AVT = YA[1][0:PAIR, 0:P]

        b1_dram = nc.dram_tensor("agent_bias_table", [PAIRS, CHUNKS, PAIR, CHUNK], F32, kind="Internal").ap()
        b2_dram = nc.dram_tensor("query_bias_table", [CHUNKS, SUB, SUBS * ALL_AGENTS], F32, kind="Internal").ap()
        x_v = a["x"].rearrange("b (t p) n -> b p t n", p=P)
        out_v = a["out"].rearrange("b (t p) n -> b p t n", p=P)

        waited = sem("waited")
        s_const = sem("consts_loaded")
        s_zero = sem("zeroed")
        s_dwb = sem("depthwise_built")
        s_bmm = sem("bias_matmul")
        s_bev = sem("bias_copied")
        s_b1_out = [sem(f"agent_bias_stored{j}") for j in range(2)]
        s_b2_out = [sem(f"query_bias_stored{j}") for j in range(2)]
        x_loaded = Count(sem("x_loaded"), 2 * CHUNKS, unit=16)
        gn_mv = Count(sem("gn_channel_stats_ready"), 5, 1)
        gn_mm = Count(sem("gn_group_stats_ready"), 5, 1)
        gn_read = Count(sem("gn_group_stats_read"), 5, 1)
        gn_ab = Count(sem("gn_scale_shift_ready"), 5, 1)
        x_norm = Count(sem("x_normalised"), HALVES, 0)
        v_norm = Count(sem("v_normalised"), HALVES, 0)
        cv_full = Count(sem("conv_bank_full"), 4 * CV_PER)
        cv_free = Count(sem("conv_bank_read"), 4 * CV_PER, 2)
        sc_full = Count(sem("score_bank_full"), PAIRS * CHUNKS + TILES)
        sc_free = Count(sem("score_bank_read"), PAIRS * CHUNKS + TILES, 2)
        tr_full = Count(sem("turn_bank_full"), 2 * CHUNKS + 2 * PAIRS * CHUNKS)
        tr_free = Count(sem("turn_bank_read"), 2 * CHUNKS + 2 * PAIRS * CHUNKS, 2)
        m2_ready = Count(sem("agents_for_q_ready"), 1)
        m1_ready = Count(sem("agents_for_k_ready"), 1)
        b1_loaded = [Count(sem(f"agent_bias_loaded{j}"), PAIRS * CHUNKS // 4, unit=16) for j in range(4)]
        b2_loaded = [Count(sem(f"query_bias_loaded{j}"), (CHUNKS + 1 - j) // 2, unit=16) for j in range(2)]
        nmx = Count(sem("agent_maximum_ready"), PAIRS)
        exp1 = Count(sem("agent_weights_ready"), PAIRS)
        pt_read = Count(sem("agent_weights_tile_read"), PAIRS * CHUNKS, 2)
        avs = Count(sem("agent_v_copied"), PAIRS)
        avt = Count(sem("agent_v_turned"), PAIRS)
        agv = Count(sem("agent_v_ready"), PAIRS)
        q_max = Count(sem("query_maxima_ready"), CHUNKS)
        q_sub = Count(sem("query_scores_shifted"), CHUNKS)
        q_exp = Count(sem("query_weights_ready"), CHUNKS)
        q_sum = Count(sem("query_sums_ready"), CHUNKS)
        q_mul = Count(sem("query_weights_scaled"), CHUNKS)
        dw_done = Count(sem("depthwise_done"), 2 * CHUNKS, 2)
        vg_loaded = [Count(sem(f"v_rows_loaded{j}"), CHUNKS, unit=16 * 12) for j in range(2)]
        y_full = Count(sem("attention_out_summed"), 2 * CHUNKS)
        y_free = Count(sem("attention_out_copied"), 2 * CHUNKS, 2)
        xr_loaded = [Count(sem(f"x_again_loaded{j}"), (CHUNKS + 1 - j) // 2, unit=16) for j in range(2)]
        p_affine = Count(sem("projection_normalised"), CHUNKS)
        res_done = Count(sem("residual_added"), CHUNKS, 1)
        stored = Count(sem("out_stored"), CHUNKS, unit=16)
        kp_free = Count(sem("projection_stored"), 1, 1)
        step = Count(sem("vector_step"), STEPS)

        def carry(eng, i):
            if not isinstance(i, int):
                eng.sem_inc(waited, 1)

        tables_stored = [(s_b1_out[j], 16 * (PAIRS // 2)) for j in range(2)]
        tables_stored += [(s_b2_out[j], 16 * ((CHUNKS + 1 - j) // 2)) for j in range(2)]

        block = ctx.enter_context(nc.Block())

        @block.sync
        def _(sp):
            for dst, src in ((WT[:, :, :, :], a["weights"].rearrange("p (j k o) -> p j k o", j=4, k=HALVES)),
                             (CONST[:, :], a["constants"]), (PAR[:, :], a["params"]),
                             (DWC[0:96, :], a["taps"]),
                             (Q[0:BASIS_A, 0, :], a["basis"][0:BASIS_A, :]),
                             (Q[0:BASIS_B, 1, :], a["basis"][BASIS_A:, :]),
                             (KP[0:BASIS_A, 0, 0:2 * ALL_AGENTS], a["bias_coefs"][0:BASIS_A, :]),
                             (KP[0:BASIS_B, 1, 0:2 * ALL_AGENTS], a["bias_coefs"][BASIS_A:, :])):
                sp.dma_start(dst, src).then_inc(s_const, 16)

            def load_x(i, c):
                for t in range(HALVES):
                    n = slice(c * CHUNK, (c + 1) * CHUNK)
                    sp.dma_start(X[:, t, n], x_v[i][:, t, n]).then_inc(x_loaded.sem, 16)

            for c in range(CHUNKS):
                load_x(0, c)
            sp.wait_ge(s_zero, 7)
            for p in range(PAIRS):
                sp.wait_ge(s_bev, CHUNKS * (p + 1))
                sp.dma_start(b1_dram[p].rearrange("c r n -> r c n"),
                             R1[0:PAIR, p % 2, :].rearrange("r (c n) -> r c n", c=CHUNKS)).then_inc(s_b1_out[p % 2], 16)
            for c in range(CHUNKS):
                sp.wait_ge(s_bev, PAIRS * CHUNKS + SUBS * (c + 1))
                sp.dma_start(b2_dram[c], R2[0:SUB, (c % 2) * 1792:(c % 2) * 1792 + SUBS * ALL_AGENTS]).then_inc(
                    s_b2_out[c % 2], 16)
            for s, n in tables_stored:
                sp.wait_ge(s, n)

            def image(i, prefetch):
                def rows(c):
                    for t in range(HALVES):
                        n = 2 * c + t
                        if c == 0:
                            sp.wait_ge(v_norm.sem, v_norm.at(i, t + 1))
                            carry(sp, i)
                        sp.wait_ge(dw_done.sem, dw_done.at(i, n + 1 - 2))
                        carry(sp, i)
                        for s in range(3):
                            for q in range(4):
                                sp.dma_start(VG[32 * s:32 * s + 32, t, q, :],
                                             V[32 * q:32 * q + 32, t, (ROWS * c + s) * W:(ROWS * c + s) * W + CHUNK]
                                             ).then_inc(vg_loaded[t].sem, 16)

                for n in range(PAIRS * CHUNKS):
                    p, c = n // CHUNKS, n % CHUNKS
                    if n >= 4:
                        sp.wait_ge(sc_free.sem, sc_free.at(i, n - 4 + 1))
                        carry(sp, i)
                    sp.dma_start(B1[0:PAIR, n % 4, :], b1_dram[p, c]).then_inc(b1_loaded[n % 4].sem, 16)
                    if n == 6:
                        rows(0)
                    if prefetch and n == 8:
                        sp.wait_ge(cv_full.sem, cv_full.at(i, CV_P))
                        carry(sp, i)
                    if prefetch and 8 <= n < 8 + CHUNKS:
                        load_x(i + 1, n - 8)
                for c in range(CHUNKS):
                    if c == 0:
                        sp.wait_ge(tr_full.sem, tr_full.at(i, TR_P2))
                        carry(sp, i)
                    if c >= 2:
                        sp.wait_ge(sc_free.sem, sc_free.at(i, PAIRS * CHUNKS + SUBS * (c - 1)))
                        carry(sp, i)
                    sp.dma_start(B2[0:SUB, c % 2, :], b2_dram[c]).then_inc(b2_loaded[c % 2].sem, 16)
                    if c:
                        rows(c)
                for c in range(CHUNKS):
                    sp.wait_ge(res_done.sem, res_done.at(i, c + 1 - 2 if c >= 2 else 0))
                    carry(sp, i)
                    sp.dma_start(XR[:, c % 2, :, :], x_v[i][:, :, c * CHUNK:(c + 1) * CHUNK]).then_inc(
                        xr_loaded[c % 2].sem, 16)
                    if c >= 1:
                        store(i, c - 1)
                store(i, CHUNKS - 1)
                sp.wait_ge(stored.sem, stored.at(i, CHUNKS))
                carry(sp, i)
                sp.sem_inc(kp_free.sem, 1)

            def store(i, c):
                sp.wait_ge(res_done.sem, res_done.at(i, c + 1))
                carry(sp, i)
                sp.dma_start(out_v[i][:, :, c * CHUNK:(c + 1) * CHUNK], KP[:, :, c * CHUNK:(c + 1) * CHUNK]).then_inc(
                    stored.sem, 16)

            if B > 1:
                with sp.Fori(0, B - 1) as i:
                    image(i, True)
            image(B - 1, False)

        @block.gpsimd
        def _(pool):
            pool.sem_inc(kp_free.sem, 1)

            def norm_x(i, n):
                for t in range(HALVES):
                    if t == 0:
                        pool.wait_ge(gn_ab.sem, gn_ab.at(i, n))
                        carry(pool, i)
                    pool.tensor_scalar(X[:, t, :], X[:, t, :], AB[:, GN_X, 0, t:t + 1], AB[:, GN_X, 1, t:t + 1],
                                       ALU.mult, ALU.add).then_inc(x_norm.sem, 1)

            norm_x(0, 0)

            def image(i, prefetch):
                for t in range(HALVES):
                    if t == 0:
                        pool.wait_ge(gn_ab.sem, gn_ab.at(i, 1 + GN_V))
                        carry(pool, i)
                    v_in = V_IN[:, t, :]
                    pool.tensor_scalar(v_in, v_in, AB[:, GN_V, 0, t:t + 1], AB[:, GN_V, 1, t:t + 1],
                                       ALU.mult, ALU.add).then_inc(v_norm.sem, 1)

                def shift(c):
                    t2 = T2[0:SUB, c % 2, :].rearrange("p (m a) -> p m a", a=AGENTS)
                    pool.wait_ge(q_max.sem, q_max.at(i, c + 1))
                    pool.tensor_tensor(t2, t2, QM[0:SUB, c % 2, :].unsqueeze(2).broadcast_to([SUB, SUBS * HEADS, AGENTS]),
                                       ALU.subtract).then_inc(q_sub.sem, 1)

                def scale(c):
                    t2 = T2[0:SUB, c % 2, :].rearrange("p (m a) -> p m a", a=AGENTS)
                    pool.wait_ge(q_sum.sem, q_sum.at(i, c + 1))
                    pool.tensor_tensor(t2, t2, QS[0:SUB, c % 2, :].unsqueeze(2).broadcast_to([SUB, SUBS * HEADS, AGENTS]),
                                       ALU.mult).then_inc(q_mul.sem, 1)

                shift(0)
                for c in range(CHUNKS):
                    scale(c)
                    if c + 1 < CHUNKS:
                        shift(c + 1)
                    if c == 0 and prefetch:
                        norm_x(i, 1 + GN_X)
                for c in range(CHUNKS):
                    pool.wait_ge(p_affine.sem, p_affine.at(i, c + 1))
                    pool.wait_ge(xr_loaded[c % 2].sem, xr_loaded[c % 2].at(i, c // 2 + 1))
                    kp = KP[:, :, c * CHUNK:(c + 1) * CHUNK]
                    pool.tensor_tensor(kp, kp, XR[:, c % 2, :, :], ALU.add).then_inc(res_done.sem, 1)

            if B > 1:
                with pool.Fori(0, B - 1) as i:
                    image(i, True)
            image(B - 1, False)

        @block.scalar
        def _(act):
            for s, credit in ((cv_free.sem, 2), (tr_free.sem, 2), (y_free.sem, 2)):
                act.sem_inc(s, credit)
            act.wait_ge(s_zero, 7)
            for n in range(PAIRS * CHUNKS + TILES):
                act.wait_ge(s_bmm, n + 1)
                if n < PAIRS * CHUNKS:
                    p, c = n // CHUNKS, n % CHUNKS
                    if p >= 2 and c == 0:
                        act.wait_ge(s_b1_out[p % 2], 16 * (p // 2))
                    act.copy(R1[0:PAIR, p % 2, c * CHUNK:(c + 1) * CHUNK], SC[n % 2][0:PAIR, 0:CHUNK]).then_inc(s_bev, 1)
                else:
                    c, s = (n - PAIRS * CHUNKS) // SUBS, n % SUBS
                    if c >= 2 and s == 0:
                        act.wait_ge(s_b2_out[c % 2], 16 * (c // 2))
                    at = (c % 2) * 1792 + s * ALL_AGENTS
                    act.copy(R2[0:SUB, at:at + ALL_AGENTS], SC[n % 2][0:SUB, 0:ALL_AGENTS]).then_inc(s_bev, 1)
            for s, n in tables_stored:
                act.wait_ge(s, n)

            def image(i, prefetch):
                def conv_out(first, dst):
                    for c in range(CHUNKS):
                        for t in range(HALVES):
                            n = first + 2 * c + t
                            act.wait_ge(cv_full.sem, cv_full.at(i, n + 1))
                            act.copy(dst[:, t, c * CHUNK:(c + 1) * CHUNK], CV[n % 2][:, 0:CHUNK]).then_inc(cv_free.sem, 1)

                def turned(n, dst):
                    act.wait_ge(tr_full.sem, tr_full.at(i, n + 1))
                    act.copy(dst, TR[n % 2][0:dst.shape[0], 0:dst.shape[1] * dst.shape[2]].rearrange(
                        "p (u m) -> p u m", u=dst.shape[1])).then_inc(tr_free.sem, 1)

                conv_out(CV_Q, Q)
                conv_out(CV_V, V_IN)
                act.wait_ge(kp_free.sem, kp_free.at(i, 0))
                conv_out(CV_K, KP)

                def vt(t):
                    if t:
                        act.wait_ge(pt_read.sem, pt_read.at(i, 2 * CHUNKS))
                    for u in range(CHUNKS):
                        turned(TR_VT[t] + u, VT[:, SUBS * u:SUBS * (u + 1), :])

                def weights(p):
                    act.wait_ge(nmx.sem, nmx.at(i, p + 1))
                    act.activation(T1[0:PAIR, p % 2, :], T1[0:PAIR, p % 2, :], ACT.Exp, bias=NM[0:PAIR, p:p + 1],
                                   accum_out=SUMS[0:PAIR, p:p + 1]).then_inc(exp1.sem, 1)

                vt(0)
                weights(0)
                for p in range(PAIRS):
                    if p + 1 < PAIRS:
                        weights(p + 1)
                    for u in range(CHUNKS):
                        act.wait_ge(pt_read.sem, pt_read.at(i, CHUNKS * p + u + 1 - 2))
                        turned(TR_PT[p] + u, PT[0:SUB, (CHUNKS * p + u) % 2, :].rearrange("p (u m) -> p u m", u=SUBS))
                    act.wait_ge(pt_read.sem, pt_read.at(i, CHUNKS * (p + 1)))
                    act.copy(AVS[:, :], YA[0][:, 0:PAIR]).then_inc(avs.sem, 1)
                    if p == 1:
                        vt(1)

                def query_weights(c):
                    act.wait_ge(q_sub.sem, q_sub.at(i, c + 1))
                    act.activation(T2[0:SUB, c % 2, :], T2[0:SUB, c % 2, :], ACT.Exp).then_inc(q_exp.sem, 1)

                def projection_out(c):
                    for t in range(HALVES):
                        n = CV_P + 2 * c + t
                        act.wait_ge(cv_full.sem, cv_full.at(i, n + 1))
                        act.copy(KP[:, t, c * CHUNK:(c + 1) * CHUNK], CV[n % 2][:, 0:CHUNK]).then_inc(cv_free.sem, 1)

                query_weights(0)
                for c in range(CHUNKS):
                    if c >= 2:
                        act.wait_ge(y_full.sem, y_full.at(i, 2 * (c - 1)))
                    for p in range(PAIRS):
                        n = TR_P2 + PAIRS * c + p
                        act.wait_ge(tr_full.sem, tr_full.at(i, n + 1))
                        act.copy(P2[0:PAIR, c % 2, p, :], TR[n % 2][0:PAIR, 0:CHUNK]).then_inc(tr_free.sem, 1)
                    for t in range(HALVES):
                        act.wait_ge(y_full.sem, y_full.at(i, 2 * c + t + 1))
                        if t == 0 and c >= 2:
                            act.wait_ge(cv_full.sem, cv_full.at(i, CV_P + 2 * (c - 1)))
                        act.activation(Y[:, c % 2, t, :], YA[t][:, 0:CHUNK], ACT.Identity,
                                       bias=dwc_b[:, t:t + 1]).then_inc(y_free.sem, 1)
                    if c:
                        projection_out(c - 1)
                    if c + 1 < CHUNKS:
                        query_weights(c + 1)
                projection_out(CHUNKS - 1)
                act.wait_ge(gn_ab.sem, gn_ab.at(i, 1 + (GN_P if prefetch else GN_X)))
                for c in range(CHUNKS):
                    for t in range(HALVES):
                        kp = KP[:, t, c * CHUNK:(c + 1) * CHUNK]
                        last = act.activation(kp, kp, ACT.Identity, bias=AB[:, GN_P, 1, t:t + 1],
                                              scale=AB[:, GN_P, 0, t:t + 1])
                    last.then_inc(p_affine.sem, 1)

            if B > 1:
                with act.Fori(0, B - 1) as i:
                    image(i, True)
            image(B - 1, False)

        @block.vector
        def _(dve):
            for s, credit in ((sc_free.sem, 2), (res_done.sem, 1)):
                dve.sem_inc(s, credit)
            for n, z in enumerate((V[:, :, :], DW[:, :, :, :], M1[:, :, :], M2[:, :, :], AGV[:, :, :], VG[:, :, :, :])):
                dve.memset(z, 0.0).then_inc(s_zero, 1)
            dve.memset(R2[:, :], 0.0).then_inc(s_zero, 1)
            dve.wait_ge(s_zero, 7)
            dve.wait_ge(s_const, 16 * 8)
            for g in range(PATCHES):
                for dx in range(3):
                    last = dve.tensor_scalar(DW[0:96, g, dx, :], eye32[0:96, :], DWC[0:96, g * 3 + dx:g * 3 + dx + 1],
                                             None, ALU.mult)
            last.then_inc(s_dwb, 1)

            taken = [0]

            def chain(i, ins):
                taken[0] += 1
                ins.then_inc(step.sem, 1)
                dve.wait_ge(step.sem, step.at(i, taken[0]))
                carry(dve, i)

            def norm_coefs(i, which, k, before):
                chain(i, before)
                for t in range(HALVES):
                    last = dve.bn_aggr(MV[:, t, :], ST[:, t, :, :].rearrange("p c s -> p (c s)"))
                chain(i, last)
                chain(i, dve.tensor_tensor(SQ[:, :], MV[:, :, 0], MV[:, :, 0], ALU.mult))
                dve.tensor_tensor(MV[:, :, 1], MV[:, :, 1], SQ[:, :], ALU.add).then_inc(gn_mv.sem, 1)
                dve.wait_ge(gn_mm.sem, gn_mm.at(i, k))
                carry(dve, i)
                chain(i, dve.tensor_copy(GS[:, :, :], MISC.rearrange("p (t k) -> p t k", t=HALVES)))
                chain(i, dve.tensor_tensor(SQ[:, :], GS[:, :, 0], GS[:, :, 0], ALU.mult))
                dve.tensor_tensor(VAR[:, :], GS[:, :, 1], SQ[:, :], ALU.subtract).then_inc(gn_read.sem, 1)
                dve.wait_ge(gn_read.sem, gn_read.at(i, k))
                carry(dve, i)
                chain(i, dve.tensor_scalar(VAR[:, :], VAR[:, :], 0.0, EPS, ALU.max, ALU.add))
                dve.tensor_scalar(MINUS_HALF[:, :], VAR[:, :], -0.5, None, ALU.mult)
                chain(i, dve.tensor_scalar(HALF_BITS[:, :], VAR[:, :].bitcast(mybir.dt.int32), 1, None,
                                           ALU.logical_shift_right))
                chain(i, dve.tensor_scalar(RS[:, :].bitcast(mybir.dt.int32), HALF_BITS[:, :], -1.0, RSQRT_GUESS,
                                           ALU.mult, ALU.add))
                for _ in range(NEWTON):
                    chain(i, dve.tensor_tensor(SQ[:, :], RS[:, :], RS[:, :], ALU.mult))
                    chain(i, dve.tensor_tensor(SQ[:, :], SQ[:, :], MINUS_HALF[:, :], ALU.mult))
                    chain(i, dve.scalar_tensor_tensor(out=RS[:, :], in0=SQ[:, :], scalar=1.5, in1=RS[:, :],
                                                      op0=ALU.add, op1=ALU.mult))
                if which == GN_X:
                    chain(i, dve.tensor_copy(AB[:, which, 0, :], RS[:, :]))
                else:
                    chain(i, dve.tensor_tensor(AB[:, which, 0, :], RS[:, :], gn_par[:, which, 0, :], ALU.mult))
                chain(i, dve.tensor_tensor(SQ[:, :], GS[:, :, 0], AB[:, which, 0, :], ALU.mult))
                if which == GN_X:
                    dve.tensor_scalar(AB[:, which, 1, :], SQ[:, :], -1.0, None, ALU.mult).then_inc(gn_ab.sem, 1)
                else:
                    dve.tensor_tensor(AB[:, which, 1, :], gn_par[:, which, 1, :], SQ[:, :], ALU.subtract).then_inc(
                        gn_ab.sem, 1)

            def x_stats(i, k):
                for t in range(HALVES):
                    for c in range(CHUNKS):
                        last = dve.bn_stats(ST[:, t, c, :], X[:, t, c * CHUNK:(c + 1) * CHUNK])
                return last

            def conv_stats(i, first, src):
                for c in range(CHUNKS):
                    for t in range(HALVES):
                        dve.wait_ge(cv_free.sem, cv_free.at(i, first + 2 * c + t + 1))
                        last = dve.bn_stats(ST[:, t, c, :], src[:, t, c * CHUNK:(c + 1) * CHUNK])
                return last

            dve.wait_ge(x_loaded.sem, x_loaded.at(0, 2 * CHUNKS))
            norm_coefs(0, GN_X, 0, x_stats(0, 0))
            first_steps = taken[0]

            def image(i, prefetch):
                taken[0] = first_steps
                norm_coefs(i, GN_Q, 1 + GN_Q, conv_stats(i, CV_Q, Q))
                dve.wait_ge(gn_ab.sem, gn_ab.at(i, 1 + GN_Q))
                for t in range(HALVES):
                    last = dve.tensor_scalar(Q[:, t, :], Q[:, t, :], AB[:, GN_Q, 0, t:t + 1], AB[:, GN_Q, 1, t:t + 1],
                                             ALU.mult, ALU.add)
                chain(i, last)
                for t in range(HALVES):
                    last = dve.tensor_reduce(
                        AG[:, t, :].rearrange("p (y x) -> p y x", x=GRID),
                        Q[:, t, :].rearrange("p (y r x s) -> p y x r s", y=GRID, r=CELL, x=GRID), AX.XY, ALU.add)
                chain(i, last)
                for h in range(HALF_HEADS):
                    rows = slice(HEAD_DIM * h, HEAD_DIM * (h + 1))
                    last = dve.tensor_scalar(M2[rows, :, AGENTS * h:AGENTS * (h + 1)], AG[rows, :, :],
                                             SCALE / CELL ** 2, None, ALU.mult)
                last.then_inc(m2_ready.sem, 1)

                norm_coefs(i, GN_V, 1 + GN_V, conv_stats(i, CV_V, V_IN))
                norm_coefs(i, GN_K, 1 + GN_K, conv_stats(i, CV_K, KP))
                dve.wait_ge(gn_ab.sem, gn_ab.at(i, 1 + GN_K))
                for t in range(HALVES):
                    last = dve.tensor_scalar(M1[:, t, :], M2[:, t, :], AB[:, GN_K, 0, t:t + 1], None, ALU.mult)
                last.then_inc(m1_ready.sem, 1)

                def agent_scores(p):
                    for c in range(CHUNKS):
                        n = CHUNKS * p + c
                        dve.wait_ge(sc_full.sem, sc_full.at(i, n + 1))
                        carry(dve, i)
                        dve.wait_ge(b1_loaded[n % 4].sem, b1_loaded[n % 4].at(i, n // 4 + 1))
                        carry(dve, i)
                        if c == 0 and p >= 2:
                            dve.wait_ge(pt_read.sem, pt_read.at(i, CHUNKS * (p - 1)))
                            carry(dve, i)
                        last = dve.tensor_tensor_reduce(
                            T1[0:PAIR, p % 2, c * CHUNK:(c + 1) * CHUNK], SC[n % 2][0:PAIR, 0:CHUNK],
                            B1[0:PAIR, n % 4, :], 1.0, -3.0e38, ALU.add, ALU.max, MX[0:PAIR, c:c + 1])
                        last.then_inc(sc_free.sem, 1)
                    dve.wait_ge(sc_free.sem, sc_free.at(i, CHUNKS * (p + 1)))
                    chain(i, dve.tensor_reduce(MAX[0:PAIR, p:p + 1], MX[0:PAIR, :], AX.X, ALU.max))
                    dve.tensor_scalar(NM[0:PAIR, p:p + 1], MAX[0:PAIR, p:p + 1], -1.0, None, ALU.mult).then_inc(
                        nmx.sem, 1)

                def agent_values(p):
                    dve.wait_ge(avt.sem, avt.at(i, p + 1))
                    chain(i, dve.reciprocal(SUMS[0:PAIR, p:p + 1], SUMS[0:PAIR, p:p + 1]))
                    at = 2 * HEAD_DIM * (p % 2)
                    dve.scalar_tensor_tensor(out=AGV[0:PAIR, p, :], in0=AVT[:, at:at + 2 * HEAD_DIM],
                                             scalar=SUMS[0:PAIR, p:p + 1], in1=pair_mask[0:PAIR, :],
                                             op0=ALU.mult, op1=ALU.mult).then_inc(agv.sem, 1)

                def query_scores(c):
                    for s in range(SUBS):
                        n = PAIRS * CHUNKS + SUBS * c + s
                        dve.wait_ge(sc_full.sem, sc_full.at(i, n + 1))
                        if s == 0:
                            if c == 0:
                                dve.wait_ge(pt_read.sem, pt_read.at(i, 3 * CHUNKS))
                            if c >= 2:
                                dve.wait_ge(tr_full.sem, tr_full.at(i, TR_P2 + PAIRS * (c - 1)))
                            dve.wait_ge(b2_loaded[c % 2].sem, b2_loaded[c % 2].at(i, c // 2 + 1))
                        m = slice(s * ALL_AGENTS, (s + 1) * ALL_AGENTS)
                        last = dve.tensor_tensor(T2[0:SUB, c % 2, m], SC[n % 2][0:SUB, 0:ALL_AGENTS],
                                                 B2[0:SUB, c % 2, m], ALU.add)
                        last.then_inc(sc_free.sem, 1)
                    dve.wait_ge(sc_free.sem, sc_free.at(i, PAIRS * CHUNKS + SUBS * (c + 1)))
                    dve.tensor_reduce(QM[0:SUB, c % 2, :], T2[0:SUB, c % 2, :].rearrange("p (m a) -> p m a", a=AGENTS),
                                      AX.X, ALU.max).then_inc(q_max.sem, 1)

                def query_sums(c):
                    dve.wait_ge(q_exp.sem, q_exp.at(i, c + 1))
                    chain(i, dve.tensor_reduce(QS[0:SUB, c % 2, :],
                                               T2[0:SUB, c % 2, :].rearrange("p (m a) -> p m a", a=AGENTS),
                                               AX.X, ALU.add))
                    dve.reciprocal(QS[0:SUB, c % 2, :], QS[0:SUB, c % 2, :]).then_inc(q_sum.sem, 1)

                agent_scores(0)
                agent_scores(1)
                agent_scores(2)
                agent_values(0)
                agent_scores(3)
                agent_values(1)
                agent_values(2)
                query_scores(0)
                agent_values(3)
                if prefetch:
                    dve.wait_ge(x_loaded.sem, x_loaded.at(i + 1, 2 * CHUNKS))
                    norm_coefs(i, GN_X, 1 + GN_X, x_stats(i, 1 + GN_X))
                for c in range(CHUNKS):
                    query_sums(c)
                    if c + 1 < CHUNKS:
                        query_scores(c + 1)
                    if c:
                        for t in range(HALVES):
                            dve.wait_ge(cv_free.sem, cv_free.at(i, CV_P + 2 * (c - 1) + t + 1))
                            dve.bn_stats(ST[:, t, c - 1, :], KP[:, t, (c - 1) * CHUNK:c * CHUNK])
                for t in range(HALVES):
                    dve.wait_ge(cv_free.sem, cv_free.at(i, CV_P + 2 * (CHUNKS - 1) + t + 1))
                    last = dve.bn_stats(ST[:, t, CHUNKS - 1, :], KP[:, t, (CHUNKS - 1) * CHUNK:])
                norm_coefs(i, GN_P, 1 + (GN_P if prefetch else GN_X), last)
                if prefetch:
                    assert taken[0] - first_steps == STEPS, taken[0] - first_steps

            if B > 1:
                with dve.Fori(0, B - 1) as i:
                    image(i, True)
            image(B - 1, False)

        @block.tensor
        def _(pe):
            for s, credit in ((dw_done.sem, 2), (pt_read.sem, 2)):
                pe.sem_inc(s, credit)
            pe.wait_ge(s_const, 16 * 8)
            for n in range(PAIRS * CHUNKS + TILES):
                if n >= 2:
                    pe.wait_ge(s_bev, n - 1)
                if n < PAIRS * CHUNKS:
                    p, c = n // CHUNKS, n % CHUNKS
                    for half, k in ((0, BASIS_A), (1, BASIS_B)):
                        last = pe.matmul(SC[n % 2][0:PAIR, 0:CHUNK], KP[0:k, half, PAIR * p:PAIR * (p + 1)],
                                         Q[0:k, half, c * CHUNK:(c + 1) * CHUNK], start=(half == 0), stop=(half == 1))
                else:
                    u = n - PAIRS * CHUNKS
                    for half, k in ((0, BASIS_A), (1, BASIS_B)):
                        last = pe.matmul(SC[n % 2][0:SUB, 0:ALL_AGENTS], Q[0:k, half, SUB * u:SUB * (u + 1)],
                                         KP[0:k, half, ALL_AGENTS:2 * ALL_AGENTS], start=(half == 0), stop=(half == 1))
                last.then_inc(s_bmm, 1)

            def group_stats(i, k):
                pe.wait_ge(gn_mv.sem, gn_mv.at(i, k))
                pe.matmul(MISC, group_mean, MV[:, :, :].rearrange("p t k -> p (t k)"), start=True, stop=True).then_inc(
                    gn_mm.sem, 1)

            pe.wait_ge(s_dwb, 1)
            group_stats(0, 0)

            def image(i, prefetch):
                def conv(first, j, c, rhs, signal=None):
                    for t in range(HALVES):
                        n = first + 2 * c + t
                        pe.wait_ge(cv_free.sem, cv_free.at(i, n + 1 - 2))
                        for k in range(HALVES):
                            last = pe.matmul(CV[n % 2][:, 0:CHUNK], WT[:, j, k, t * P:(t + 1) * P], rhs(c, k),
                                             start=(k == 0), stop=(k == HALVES - 1))
                        last.then_inc(cv_full.sem, 1)
                x_in = lambda c, k: X[:, k, c * CHUNK:(c + 1) * CHUNK]

                pe.wait_ge(x_norm.sem, x_norm.at(i, 2))
                for c in range(CHUNKS):
                    conv(CV_Q, 0, c, x_in)
                for c in range(CHUNKS):
                    conv(CV_V, 1, c, x_in)
                    if c == 3:
                        group_stats(i, 1 + GN_Q)
                for c in range(CHUNKS):
                    conv(CV_K, 2, c, x_in)
                    if c == 3:
                        group_stats(i, 1 + GN_V)

                def turn_v(t):
                    for u in range(CHUNKS):
                        n = TR_VT[t] + u
                        pe.wait_ge(tr_free.sem, tr_free.at(i, n + 1 - 2))
                        for s in range(SUBS):
                            v = V_IN[:, t, SUB * (SUBS * u + s):SUB * (SUBS * u + s + 1)]
                            last = pe.transpose(TR[n % 2][0:SUB, s * P:(s + 1) * P], v, ident)
                        last.then_inc(tr_full.sem, 1)

                pe.wait_ge(v_norm.sem, v_norm.at(i, 2))
                turn_v(0)
                group_stats(i, 1 + GN_K)

                def agent_scores(p):
                    for c in range(CHUNKS):
                        n = CHUNKS * p + c
                        pe.wait_ge(sc_free.sem, sc_free.at(i, n + 1 - 2))
                        pe.matmul(SC[n % 2][0:PAIR, 0:CHUNK], M1[:, p // 2, PAIR * (p % 2):PAIR * (p % 2 + 1)],
                                  KP[:, p // 2, c * CHUNK:(c + 1) * CHUNK], start=True, stop=True).then_inc(sc_full.sem, 1)

                def agent_sum(p, c):
                    pe.wait_ge(tr_free.sem, tr_free.at(i, TR_PT[p] + c + 1))
                    for s in range(SUBS):
                        u = SUBS * c + s
                        last = pe.matmul(YA[0][:, 0:PAIR], VT[:, u, :],
                                         PT[0:SUB, (CHUNKS * p + c) % 2, PAIR * s:PAIR * (s + 1)],
                                         start=(u == 0), stop=(u == TILES - 1))
                    last.then_inc(pt_read.sem, 1)

                def agent_out(p):
                    pe.wait_ge(exp1.sem, exp1.at(i, p + 1))
                    if p:
                        pe.wait_ge(avs.sem, avs.at(i, p))
                    for c in range(CHUNKS):
                        n = TR_PT[p] + c
                        pe.wait_ge(tr_free.sem, tr_free.at(i, n + 1 - 2))
                        for s in range(SUBS):
                            u = SUBS * c + s
                            last = pe.transpose(TR[n % 2][0:SUB, PAIR * s:PAIR * (s + 1)],
                                                T1[0:PAIR, p % 2, SUB * u:SUB * (u + 1)], ident[0:PAIR, 0:PAIR])
                        last.then_inc(tr_full.sem, 1)
                        if c:
                            agent_sum(p, c - 1)
                    agent_sum(p, CHUNKS - 1)

                def turn_agent_v(p):
                    pe.wait_ge(avs.sem, avs.at(i, p + 1))
                    if p:
                        pe.wait_ge(agv.sem, agv.at(i, p))
                    pe.transpose(AVT, AVS[:, :], ident).then_inc(avt.sem, 1)

                def query_scores(c):
                    for s in range(SUBS):
                        u = SUBS * c + s
                        n = PAIRS * CHUNKS + u
                        pe.wait_ge(sc_free.sem, sc_free.at(i, n + 1 - 2))
                        for t in range(HALVES):
                            last = pe.matmul(SC[n % 2][0:SUB, HALF_AGENTS * t:HALF_AGENTS * (t + 1)],
                                             Q[:, t, SUB * u:SUB * (u + 1)], M2[:, t, :], start=True, stop=True)
                        last.then_inc(sc_full.sem, 1)

                pe.wait_ge(m1_ready.sem, m1_ready.at(i, 1))
                agent_scores(0)
                agent_scores(1)
                agent_out(0)
                agent_scores(2)
                turn_agent_v(0)
                agent_out(1)
                turn_v(1)
                agent_scores(3)
                turn_agent_v(1)
                agent_out(2)
                turn_agent_v(2)
                agent_out(3)
                query_scores(0)
                turn_agent_v(3)
                pe.wait_ge(agv.sem, agv.at(i, PAIRS))
                if prefetch:
                    group_stats(i, 1 + GN_X)
                    pe.wait_ge(gn_read.sem, gn_read.at(i, 1 + GN_X))

                def depthwise(c, t):
                    pe.wait_ge(vg_loaded[t].sem, vg_loaded[t].at(i, c + 1))
                    pe.wait_ge(y_free.sem, y_free.at(i, 2 * c + t + 1 - 2))
                    for dx, to, of in ((1, 0, 0), (0, 1, 0), (2, 0, 1)):
                        w = W if dx == 1 else W - 1
                        for q in range(4):
                            out = YA[t][32 * q:32 * (q + 1), 0:CHUNK].rearrange("p (h w) -> p h w", w=W)[:, :, to:to + w]
                            rows = VG[:, t, q, :].rearrange("p (h w) -> p h w", w=W)[:, :, of:of + w]
                            last = pe.matmul(out, DW[:, 4 * t + q, dx, :], rows, start=(dx == 1), stop=False,
                                             skip_group_check=True)
                    last.then_inc(dw_done.sem, 1)

                def turn_query(c):
                    pe.wait_ge(q_mul.sem, q_mul.at(i, c + 1))
                    for p in range(PAIRS):
                        n = TR_P2 + PAIRS * c + p
                        pe.wait_ge(tr_free.sem, tr_free.at(i, n + 1 - 2))
                        for s in range(SUBS):
                            m = s * ALL_AGENTS + PAIR * p
                            last = pe.transpose(TR[n % 2][0:PAIR, SUB * s:SUB * (s + 1)],
                                                T2[0:SUB, c % 2, m:m + PAIR], ident[0:SUB, 0:SUB])
                        last.then_inc(tr_full.sem, 1)

                def attend(c):
                    for t in range(HALVES):
                        pe.wait_ge(tr_free.sem, tr_free.at(i, TR_P2 + PAIRS * c + 2 * t + 2))
                        for g in range(2):
                            last = pe.matmul(YA[t][64 * g:64 * (g + 1), 0:CHUNK], AGV[:, 2 * t + g, :],
                                             P2[:, c % 2, 2 * t + g, :], start=False, stop=True, skip_group_check=True)
                        last.then_inc(y_full.sem, 1)

                def project(c):
                    pe.wait_ge(y_free.sem, y_free.at(i, 2 * (c + 1)))
                    conv(CV_P, 3, c, lambda c, k: Y[:, c % 2, k, :])

                for c in range(CHUNKS):
                    if c + 1 < CHUNKS:
                        query_scores(c + 1)
                    for t in range(HALVES):
                        depthwise(c, t)
                    turn_query(c)
                    attend(c)
                    if c:
                        project(c - 1)
                project(CHUNKS - 1)
                group_stats(i, 1 + (GN_P if prefetch else GN_X))

            if B > 1:
                with pe.Fori(0, B - 1) as i:
                    image(i, True)
            image(B - 1, False)


TR_VT = [0, CHUNKS + 2 * CHUNKS]
TR_PT = [CHUNKS, 2 * CHUNKS, 4 * CHUNKS, 5 * CHUNKS]
TR_P2 = 6 * CHUNKS
STEPS = 5 * (7 + 3 + 3 * NEWTON) + 2 + PAIRS * 2 + CHUNKS


def layouts(x, p):
    B = x.shape[0]
    at = lambda n: np.asarray(p[f"L0_conv_{n}"])
    by_half = lambda v: v.reshape(HALVES, P).T
    weights = np.stack([at(f"{n}_w").T.reshape(HALVES, P, C) for n in "qvkp"])
    params = [by_half(at(f"{n}_g{k}")) for n in "qvk" for k in "wb"]
    params += [np.zeros((P, 2 * HALVES), np.float32)]
    params += [by_half(at(f"p_g{k}")) for k in "wb"] + [by_half(at("dwc_b"))]
    taps = at("dwc_w").reshape(PATCHES, HEAD_DIM, 3, 3).transpose(2, 1, 0, 3)
    coefs = np.concatenate([
        np.concatenate([at("an_bias").reshape(ALL_AGENTS, GRID * GRID).T, at("ah_bias").reshape(ALL_AGENTS, H).T,
                        at("aw_bias").reshape(ALL_AGENTS, W).T]),
        np.concatenate([at("na_bias").reshape(ALL_AGENTS, GRID * GRID).T,
                        at("ha_bias").reshape(HEADS, H, AGENTS).transpose(1, 0, 2).reshape(H, ALL_AGENTS),
                        at("wa_bias").reshape(HEADS, W, AGENTS).transpose(1, 0, 2).reshape(W, ALL_AGENTS)])], axis=1)
    where = (np.arange(H) + 0.5) / CELL - 0.5
    line = np.maximum(0, 1 - np.abs(where[None, :] - np.arange(GRID)[:, None]))
    line /= line.sum(0)
    grid = np.einsum("iy,jx->ijyx", line, line).reshape(GRID * GRID, N)
    ys = np.repeat(np.eye(H), W, axis=1)
    xs = np.tile(np.eye(W), (1, H))
    same_group = np.kron(np.eye(P // GROUP), np.ones((GROUP, GROUP))) / GROUP
    heads = np.zeros((P, 2 * HEAD_DIM))
    heads[:PAIR] = np.kron(np.eye(2), np.ones((AGENTS, HEAD_DIM)))
    constants = np.concatenate([np.eye(P), same_group, np.tile(np.eye(HEAD_DIM), (P // HEAD_DIM, 1)), heads], axis=1)
    return {
        "x": np.asarray(x).reshape(B, C, N),
        "weights": np.ascontiguousarray(weights.transpose(2, 0, 1, 3).reshape(P, 4 * HALVES * C)),
        "params": np.ascontiguousarray(np.concatenate(params, axis=1)),
        "taps": np.ascontiguousarray(taps.reshape(3 * HEAD_DIM, PATCHES * 3)),
        "bias_coefs": np.ascontiguousarray(coefs),
        "basis": np.concatenate([grid, ys, xs]).astype(np.float32),
        "constants": constants.astype(np.float32),
    }


def kernel(x, **params):
    import concourse.bacc as bacc
    from concourse.bass_utils import run_bass_kernel_spmd

    B = x.shape[0]
    arrays = layouts(x, params)
    nc = bacc.Bacc("TRN2", target_bir_lowering=False, num_devices=1)
    dram = {n: nc.dram_tensor(n, v.shape, F32, kind="ExternalInput").ap() for n, v in arrays.items()}
    dram["out"] = nc.dram_tensor("out", (B, C, N), F32, kind="ExternalOutput").ap()
    attention_block(nc, B, dram)
    r = run_bass_kernel_spmd(nc, [arrays], core_ids=[0])
    return r.results[0]["out"].reshape(B, C, H, W)
```

```python
from contextlib import ExitStack

import numpy as np

import concourse.bass as bass
from concourse import mybir

F32 = mybir.dt.float32
ALU = mybir.AluOpType
ACT = mybir.ActivationFunctionType
AX = mybir.AxisListType

P = 128
C = 256
HALVES = C // P
H = W = 56
N = H * W
HEADS = 8
HEAD_DIM = C // HEADS
AGENTS = 49
GRID = 7
CELL = H // GRID
PAIRS = HEADS // 2
PAIR = 2 * AGENTS
HALF_HEADS = HEADS // HALVES
HALF_AGENTS = HALF_HEADS * AGENTS
ALL_AGENTS = HEADS * AGENTS
GROUP = C // 32
SCALE = HEAD_DIM ** -0.5
EPS = 1e-5
RSQRT_GUESS = float(0x5F3759DF)
NEWTON = 3

ROWS = 8
CHUNK = ROWS * W
CHUNKS = H // ROWS
SUB = 112
SUBS = CHUNK // SUB
TILES = N // SUB
PATCHES = C // HEAD_DIM
BASIS_A = GRID * GRID + H
BASIS_B = W
PARTS = (0, (CHUNKS + 1) // 2, CHUNKS)

GN_Q, GN_K, GN_V, GN_X, GN_P = range(5)
CV_PER = 2 * CHUNKS
CV_Q, CV_K, CV_V, CV_P = (j * CV_PER for j in range(4))


class Count:

    def __init__(self, sem, per, credit=0, unit=1):
        self.sem, self.per, self.credit, self.unit = sem, per, credit, unit

    def at(self, i, k):
        return i * (self.per * self.unit) + (k * self.unit + self.credit)


def attention_block(nc, B, a):
    ctx = ExitStack()
    with ctx:
        def sb(name, shape, dt=F32):
            return ctx.enter_context(nc.sbuf_tensor("sb_" + name, shape, dt))

        def sem(name):
            return ctx.enter_context(nc.semaphore(name))

        X = sb("x_norm", [P, HALVES, N])
        Q = sb("q", [P, HALVES, N])
        KP = sb("k_then_projection", [P, HALVES, N])
        V = sb("v_padded", [P, HALVES, (H + 2) * W])
        R1 = sb("scores", [P, 2, N])
        R2 = sb("transposed", [P, 2 * PAIRS * CHUNK])
        PT = sb("agent_weights_by_position", [P, 2, SUBS * PAIR])
        VG = sb("v_three_rows", [P, 2, PATCHES // 2, CHUNK])
        B1 = sb("agent_bias", [P, 4, CHUNK])
        B2 = sb("query_bias", [P, 2, SUBS * ALL_AGENTS])
        Y = sb("attention_out", [P, 2, HALVES, CHUNK])
        XR = sb("x_again", [P, 2, HALVES, CHUNK])
        WT = sb("weights", [P, 4, HALVES, C])
        DW = sb("depthwise_diagonals", [P, PATCHES, 3, HEAD_DIM])
        CONST = sb("constants", [P, 2 * P + HEAD_DIM + 2 * HEAD_DIM])
        PAR = sb("params", [P, 5 * 2 * HALVES + HALVES])
        DWC = sb("depthwise_taps", [P, PATCHES * 3])
        M1 = sb("agents_for_k", [P, HALVES, HALF_AGENTS])
        M2 = sb("agents_for_q", [P, HALVES, HALF_AGENTS])
        AG = sb("pooled_q", [P, HALVES, AGENTS])
        AGV = sb("agent_v", [P, PAIRS, 2 * HEAD_DIM])
        AVS = sb("agent_v_channels", [P, PAIR])
        ST = sb("chunk_stats", [P, HALVES, CHUNKS, 6])
        MV = sb("channel_stats", [P, HALVES, 2])
        SQ = sb("squares", [P, HALVES])
        GS = sb("group_stats", [P, HALVES, 2])
        VAR = sb("group_variance", [P, HALVES])
        RS = sb("group_rsqrt", [P, HALVES])
        HALF_BITS = sb("halved_bits", [P, HALVES], mybir.dt.int32)
        MINUS_HALF = sb("minus_half_variance", [P, HALVES])
        AB = sb("scale_and_shift", [P, 5, 2, HALVES])
        MX = sb("chunk_maxima", [P, CHUNKS])
        MAX = sb("agent_maxima", [P, PAIRS])
        NM = sb("negative_maximum", [P, PAIRS])
        SUMS = sb("agent_sums", [P, PAIRS, 2])
        INV = sb("agent_sums_inverse", [P, PAIRS])
        QM = sb("query_maxima", [P, 2, SUBS * HEADS])
        QS = sb("query_sums", [P, 2, SUBS * HEADS])

        T1 = R1
        T2 = R1[:, 0, :].rearrange("p (s m) -> p s m", s=2)
        VT = R2[0:SUB, :].rearrange("p (n c) -> p n c", c=P)
        P2 = R2[:, :].rearrange("p (s g n) -> p s g n", s=2, g=PAIRS)
        V_IN = V[:, :, W:W + N]
        ident = CONST[:, 0:P]
        group_mean = CONST[:, P:2 * P]
        eye32 = CONST[:, 2 * P:2 * P + HEAD_DIM]
        pair_mask = CONST[:, 2 * P + HEAD_DIM:2 * P + 3 * HEAD_DIM]
        gn_par = PAR[:, 0:20].rearrange("p (n k t) -> p n k t", n=5, k=2)
        dwc_b = PAR[:, 20:22]

        CV = [ctx.enter_context(nc.psum_tensor(f"conv{j}", [P, 512], F32)) for j in range(2)]
        SC = [ctx.enter_context(nc.psum_tensor(f"score{j}", [P, 512], F32)) for j in range(2)]
        TR = [ctx.enter_context(nc.psum_tensor(f"turn{j}", [P, 512], F32)) for j in range(2)]
        YA = [ctx.enter_context(nc.psum_tensor(f"sum{j}", [P, 512], F32)) for j in range(2)]
        MISC = YA[1][:, 256:260]
        AVT = YA[1][0:PAIR, 0:P]

        b1_dram = nc.dram_tensor("agent_bias_table", [PAIRS, CHUNKS, PAIR, CHUNK], F32, kind="Internal").ap()
        b2_dram = nc.dram_tensor("query_bias_table", [CHUNKS, SUB, SUBS * ALL_AGENTS], F32, kind="Internal").ap()
        x_v = a["x"].rearrange("b (t p) n -> b p t n", p=P)
        out_v = a["out"].rearrange("b (t p) n -> b p t n", p=P)

        waited = sem("waited")
        s_const = sem("consts_loaded")
        s_zero = sem("zeroed")
        s_dwb = sem("depthwise_built")
        s_bmm = sem("bias_matmul")
        s_bev = sem("bias_copied")
        s_b1_out = [sem(f"agent_bias_stored{j}") for j in range(2)]
        s_b2_out = [sem(f"query_bias_stored{j}") for j in range(2)]
        x_loaded = Count(sem("x_loaded"), CHUNKS, unit=16)
        gn_mv = Count(sem("gn_channel_stats_ready"), 5, 1)
        gn_mm = Count(sem("gn_group_stats_ready"), 5, 1)
        gn_read = Count(sem("gn_group_stats_read"), 5, 1)
        gn_ab = Count(sem("gn_scale_shift_ready"), 5, 1)
        x_norm = Count(sem("x_normalised"), HALVES, 0)
        v_norm = Count(sem("v_normalised"), HALVES, 0)
        cv_full = Count(sem("conv_bank_full"), 4 * CV_PER)
        cv_free = Count(sem("conv_bank_read"), 4 * CV_PER, 2)
        sc_full = Count(sem("score_bank_full"), PAIRS * CHUNKS + TILES)
        sc_free = Count(sem("score_bank_read"), PAIRS * CHUNKS + TILES, 2)
        tr_full = Count(sem("turn_bank_full"), 2 * CHUNKS + 2 * PAIRS * CHUNKS)
        tr_free = Count(sem("turn_bank_read"), 2 * CHUNKS + 2 * PAIRS * CHUNKS, 2)
        m2_ready = Count(sem("agents_for_q_ready"), 1)
        m1_ready = Count(sem("agents_for_k_ready"), 1)
        b1_loaded = [Count(sem(f"agent_bias_loaded{j}"), PAIRS * CHUNKS // 4, unit=16) for j in range(4)]
        b2_loaded = [Count(sem(f"query_bias_loaded{j}"), (CHUNKS + 1 - j) // 2, unit=16) for j in range(2)]
        nmx = Count(sem("agent_maximum_ready"), PAIRS)
        exp1 = Count(sem("agent_weights_ready"), 2 * PAIRS)
        pt_read = Count(sem("agent_weights_tile_read"), PAIRS * CHUNKS, 2)
        avs = Count(sem("agent_v_copied"), PAIRS)
        avt = Count(sem("agent_v_turned"), PAIRS)
        agv = Count(sem("agent_v_ready"), PAIRS)
        q_max = Count(sem("query_maxima_ready"), CHUNKS)
        q_sub = Count(sem("query_scores_shifted"), CHUNKS)
        q_exp = Count(sem("query_weights_ready"), CHUNKS)
        q_sum = Count(sem("query_sums_ready"), CHUNKS)
        q_mul = Count(sem("query_weights_scaled"), CHUNKS)
        dw_done = Count(sem("depthwise_done"), 2 * CHUNKS, 2)
        vg_loaded = Count(sem("v_rows_loaded"), CHUNKS, unit=16 * 12)
        y_full = Count(sem("attention_out_summed"), 2 * CHUNKS)
        y_free = Count(sem("attention_out_copied"), 2 * CHUNKS, 2)
        xr_loaded = [Count(sem(f"x_again_loaded{j}"), (CHUNKS + 1 - j) // 2, unit=16) for j in range(2)]
        p_affine = Count(sem("projection_normalised"), 2 * CHUNKS)
        res_done = Count(sem("residual_added"), CHUNKS, 1)
        stored = [Count(sem(f"out_stored{c}"), 1, 1, unit=16) for c in range(CHUNKS)]
        step = Count(sem("vector_step"), STEPS)

        def carry(eng, i):
            if not isinstance(i, int):
                eng.sem_inc(waited, 1)

        tables_stored = [(s_b1_out[j], 16 * (PAIRS // 2)) for j in range(2)]
        tables_stored += [(s_b2_out[j], 16 * ((CHUNKS + 1 - j) // 2)) for j in range(2)]

        block = ctx.enter_context(nc.Block())

        @block.sync
        def _(sp):
            for dst, src in ((WT[:, :, :, :], a["weights"].rearrange("p (j k o) -> p j k o", j=4, k=HALVES)),
                             (CONST[:, :], a["constants"]), (PAR[:, :], a["params"]),
                             (DWC[0:96, :], a["taps"]),
                             (Q[0:BASIS_A, 0, :], a["basis"][0:BASIS_A, :]),
                             (Q[0:BASIS_B, 1, :], a["basis"][BASIS_A:, :]),
                             (KP[0:BASIS_A, 0, 0:2 * ALL_AGENTS], a["bias_coefs"][0:BASIS_A, :]),
                             (KP[0:BASIS_B, 1, 0:2 * ALL_AGENTS], a["bias_coefs"][BASIS_A:, :])):
                sp.dma_start(dst, src).then_inc(s_const, 16)

            def load_x(i, c):
                n = slice(c * CHUNK, (c + 1) * CHUNK)
                sp.dma_start(X[:, :, n], x_v[i][:, :, n]).then_inc(x_loaded.sem, 16)

            for c in range(CHUNKS):
                load_x(0, c)
            sp.wait_ge(s_zero, 7)
            for p in range(PAIRS):
                sp.wait_ge(s_bev, CHUNKS * (p + 1))
                sp.dma_start(b1_dram[p].rearrange("c r n -> r c n"),
                             R1[0:PAIR, p % 2, :].rearrange("r (c n) -> r c n", c=CHUNKS)).then_inc(s_b1_out[p % 2], 16)
            for c in range(CHUNKS):
                sp.wait_ge(s_bev, PAIRS * CHUNKS + SUBS * (c + 1))
                sp.dma_start(b2_dram[c], R2[0:SUB, (c % 2) * 1792:(c % 2) * 1792 + SUBS * ALL_AGENTS]).then_inc(
                    s_b2_out[c % 2], 16)
            for s, n in tables_stored:
                sp.wait_ge(s, n)

            def image(i, prefetch):
                def rows(c):
                    if c == 0:
                        sp.wait_ge(v_norm.sem, v_norm.at(i, HALVES))
                        carry(sp, i)
                    sp.wait_ge(dw_done.sem, dw_done.at(i, 2 * c))
                    carry(sp, i)
                    for s in range(3):
                        for q in range(4):
                            at = (ROWS * c + s) * W
                            sp.dma_start(VG[32 * s:32 * s + 32, :, q, :],
                                         V[32 * q:32 * q + 32, :, at:at + CHUNK]).then_inc(vg_loaded.sem, 16)

                for n in range(PAIRS * CHUNKS):
                    p, c = n // CHUNKS, n % CHUNKS
                    if n == 2 * CHUNKS:
                        rows(0)
                    if n >= 4:
                        sp.wait_ge(sc_free.sem, sc_free.at(i, n - 4 + 1))
                        carry(sp, i)
                    sp.dma_start(B1[0:PAIR, n % 4, :], b1_dram[p, c]).then_inc(b1_loaded[n % 4].sem, 16)
                    if prefetch and n == 8:
                        sp.wait_ge(cv_full.sem, cv_full.at(i, CV_P))
                        carry(sp, i)
                    if prefetch and 8 <= n < 8 + CHUNKS:
                        load_x(i + 1, n - 8)
                for c in range(CHUNKS):
                    if c >= 2:
                        sp.wait_ge(sc_free.sem, sc_free.at(i, PAIRS * CHUNKS + SUBS * (c - 1)))
                        carry(sp, i)
                    sp.dma_start(B2[0:SUB, c % 2, :], b2_dram[c]).then_inc(b2_loaded[c % 2].sem, 16)
                    if c >= 2:
                        rows(c - 1)
                rows(CHUNKS - 1)
                for c in range(CHUNKS):
                    sp.wait_ge(res_done.sem, res_done.at(i, c + 1 - 2 if c >= 2 else 0))
                    carry(sp, i)
                    sp.dma_start(XR[:, c % 2, :, :], x_v[i][:, :, c * CHUNK:(c + 1) * CHUNK]).then_inc(
                        xr_loaded[c % 2].sem, 16)
                    if c >= 1:
                        store(i, c - 1)
                store(i, CHUNKS - 1)

            def store(i, c):
                sp.wait_ge(res_done.sem, res_done.at(i, c + 1))
                carry(sp, i)
                sp.dma_start(out_v[i][:, :, c * CHUNK:(c + 1) * CHUNK], KP[:, :, c * CHUNK:(c + 1) * CHUNK]).then_inc(
                    stored[c].sem, 16)

            if B > 1:
                with sp.Fori(0, B - 1) as i:
                    image(i, True)
            image(B - 1, False)
            for c in range(CHUNKS):
                sp.wait_ge(stored[c].sem, stored[c].at(B - 1, 1))

        @block.gpsimd
        def _(pool):
            for c in range(CHUNKS):
                pool.sem_inc(stored[c].sem, 1)

            def norm_x(i, n):
                for t in range(HALVES):
                    if t == 0:
                        pool.wait_ge(gn_ab.sem, gn_ab.at(i, n))
                        carry(pool, i)
                    pool.tensor_scalar(X[:, t, :], X[:, t, :], AB[:, GN_X, 0, t:t + 1], AB[:, GN_X, 1, t:t + 1],
                                       ALU.mult, ALU.add).then_inc(x_norm.sem, 1)

            norm_x(0, 0)

            def image(i, prefetch):
                for t in range(HALVES):
                    if t == 0:
                        pool.wait_ge(gn_ab.sem, gn_ab.at(i, 1 + GN_V))
                        carry(pool, i)
                    v_in = V_IN[:, t, :]
                    pool.tensor_scalar(v_in, v_in, AB[:, GN_V, 0, t:t + 1], AB[:, GN_V, 1, t:t + 1],
                                       ALU.mult, ALU.add).then_inc(v_norm.sem, 1)

                def shift(c):
                    t2 = T2[0:SUB, c % 2, :].rearrange("p (m a) -> p m a", a=AGENTS)
                    pool.wait_ge(q_max.sem, q_max.at(i, c + 1))
                    pool.tensor_tensor(t2, t2, QM[0:SUB, c % 2, :].unsqueeze(2).broadcast_to([SUB, SUBS * HEADS, AGENTS]),
                                       ALU.subtract).then_inc(q_sub.sem, 1)

                def scale(c):
                    t2 = T2[0:SUB, c % 2, :].rearrange("p (m a) -> p m a", a=AGENTS)
                    pool.wait_ge(q_sum.sem, q_sum.at(i, c + 1))
                    pool.tensor_tensor(t2, t2, QS[0:SUB, c % 2, :].unsqueeze(2).broadcast_to([SUB, SUBS * HEADS, AGENTS]),
                                       ALU.mult).then_inc(q_mul.sem, 1)

                if prefetch:
                    norm_x(i, 1 + GN_X)
                shift(0)
                shift(1)
                for c in range(CHUNKS):
                    scale(c)
                    if c + 2 < CHUNKS:
                        shift(c + 2)
                pool.wait_ge(gn_ab.sem, gn_ab.at(i, 1 + (GN_P if prefetch else GN_X)))
                carry(pool, i)
                for c in range(CHUNKS):
                    for t in range(HALVES):
                        p_out = KP[:, t, c * CHUNK:(c + 1) * CHUNK]
                        pool.tensor_scalar(p_out, p_out, AB[:, GN_P, 0, t:t + 1], AB[:, GN_P, 1, t:t + 1],
                                           ALU.mult, ALU.add).then_inc(p_affine.sem, 1)
                    pool.wait_ge(p_affine.sem, p_affine.at(i, 2 * (c + 1)))
                    pool.wait_ge(xr_loaded[c % 2].sem, xr_loaded[c % 2].at(i, c // 2 + 1))
                    kp = KP[:, :, c * CHUNK:(c + 1) * CHUNK]
                    pool.tensor_tensor(kp, kp, XR[:, c % 2, :, :], ALU.add).then_inc(res_done.sem, 1)

            if B > 1:
                with pool.Fori(0, B - 1) as i:
                    image(i, True)
            image(B - 1, False)

        @block.scalar
        def _(act):
            for s, credit in ((cv_free.sem, 2), (tr_free.sem, 2), (y_free.sem, 2)):
                act.sem_inc(s, credit)
            act.wait_ge(s_zero, 7)
            for n in range(PAIRS * CHUNKS + TILES):
                act.wait_ge(s_bmm, n + 1)
                if n < PAIRS * CHUNKS:
                    p, c = n // CHUNKS, n % CHUNKS
                    if p >= 2 and c == 0:
                        act.wait_ge(s_b1_out[p % 2], 16 * (p // 2))
                    act.copy(R1[0:PAIR, p % 2, c * CHUNK:(c + 1) * CHUNK], SC[n % 2][0:PAIR, 0:CHUNK]).then_inc(s_bev, 1)
                else:
                    c, s = (n - PAIRS * CHUNKS) // SUBS, n % SUBS
                    if c >= 2 and s == 0:
                        act.wait_ge(s_b2_out[c % 2], 16 * (c // 2))
                    at = (c % 2) * 1792 + s * ALL_AGENTS
                    act.copy(R2[0:SUB, at:at + ALL_AGENTS], SC[n % 2][0:SUB, 0:ALL_AGENTS]).then_inc(s_bev, 1)
            for s, n in tables_stored:
                act.wait_ge(s, n)

            def image(i, prefetch):
                def conv_out(first, dst):
                    for c in range(CHUNKS):
                        for t in range(HALVES):
                            n = first + 2 * c + t
                            if first == CV_K and t == 0:
                                act.wait_ge(stored[c].sem, stored[c].at(i, 0))
                            act.wait_ge(cv_full.sem, cv_full.at(i, n + 1))
                            act.copy(dst[:, t, c * CHUNK:(c + 1) * CHUNK], CV[n % 2][:, 0:CHUNK]).then_inc(cv_free.sem, 1)

                def turned(n, dst):
                    act.wait_ge(tr_full.sem, tr_full.at(i, n + 1))
                    act.copy(dst, TR[n % 2][0:dst.shape[0], 0:dst.shape[1] * dst.shape[2]].rearrange(
                        "p (u m) -> p u m", u=dst.shape[1])).then_inc(tr_free.sem, 1)

                conv_out(CV_Q, Q)
                conv_out(CV_K, KP)
                conv_out(CV_V, V_IN)

                def vt(t):
                    if t:
                        act.wait_ge(pt_read.sem, pt_read.at(i, 2 * CHUNKS))
                    for u in range(CHUNKS):
                        turned(TR_VT[t] + u, VT[:, SUBS * u:SUBS * (u + 1), :])

                def weights(p, part):
                    act.wait_ge(nmx.sem, nmx.at(i, p + 1))
                    t1 = T1[0:PAIR, p % 2, PARTS[part] * CHUNK:PARTS[part + 1] * CHUNK]
                    act.activation(t1, t1, ACT.Exp, bias=NM[0:PAIR, p:p + 1],
                                   accum_out=SUMS[0:PAIR, p, part:part + 1]).then_inc(exp1.sem, 1)

                def query_weights(c):
                    act.wait_ge(q_sub.sem, q_sub.at(i, c + 1))
                    act.activation(T2[0:SUB, c % 2, :], T2[0:SUB, c % 2, :], ACT.Exp).then_inc(q_exp.sem, 1)

                weights(0, 0)
                weights(0, 1)
                vt(0)
                for p in range(PAIRS):
                    for u in range(CHUNKS):
                        if u in (2, 4) and p + 1 < PAIRS:
                            weights(p + 1, u // 2 - 1)
                        elif u == 5 and p + 1 == PAIRS:
                            query_weights(0)
                        act.wait_ge(pt_read.sem, pt_read.at(i, CHUNKS * p + u + 1 - 2))
                        turned(TR_PT[p] + u, PT[0:SUB, (CHUNKS * p + u) % 2, :].rearrange("p (u m) -> p u m", u=SUBS))
                    act.wait_ge(pt_read.sem, pt_read.at(i, CHUNKS * (p + 1)))
                    act.copy(AVS[:, :], YA[0][:, 0:PAIR]).then_inc(avs.sem, 1)
                    if p == 1:
                        vt(1)

                def projection_out(c):
                    for t in range(HALVES):
                        n = CV_P + 2 * c + t
                        act.wait_ge(cv_full.sem, cv_full.at(i, n + 1))
                        act.copy(KP[:, t, c * CHUNK:(c + 1) * CHUNK], CV[n % 2][:, 0:CHUNK]).then_inc(cv_free.sem, 1)

                for c in range(CHUNKS):
                    if c + 1 < CHUNKS:
                        query_weights(c + 1)
                    if c >= 2:
                        act.wait_ge(y_full.sem, y_full.at(i, 2 * (c - 1)))
                    for p in range(PAIRS):
                        n = TR_P2 + PAIRS * c + p
                        act.wait_ge(tr_full.sem, tr_full.at(i, n + 1))
                        act.copy(P2[0:PAIR, c % 2, p, :], TR[n % 2][0:PAIR, 0:CHUNK]).then_inc(tr_free.sem, 1)
                    for t in range(HALVES):
                        act.wait_ge(y_full.sem, y_full.at(i, 2 * c + t + 1))
                        if t == 0 and c >= 2:
                            act.wait_ge(cv_full.sem, cv_full.at(i, CV_P + 2 * (c - 1)))
                        act.activation(Y[:, c % 2, t, :], YA[t][:, 0:CHUNK], ACT.Identity,
                                       bias=dwc_b[:, t:t + 1]).then_inc(y_free.sem, 1)
                    if c:
                        projection_out(c - 1)
                projection_out(CHUNKS - 1)

            if B > 1:
                with act.Fori(0, B - 1) as i:
                    image(i, True)
            image(B - 1, False)

        @block.vector
        def _(dve):
            for s, credit in ((sc_free.sem, 2), (res_done.sem, 1)):
                dve.sem_inc(s, credit)
            for n, z in enumerate((V[:, :, :], DW[:, :, :, :], M1[:, :, :], M2[:, :, :], AGV[:, :, :], VG[:, :, :, :])):
                dve.memset(z, 0.0).then_inc(s_zero, 1)
            dve.memset(R2[:, :], 0.0).then_inc(s_zero, 1)
            dve.wait_ge(s_zero, 7)
            dve.wait_ge(s_const, 16 * 8)
            for g in range(PATCHES):
                for dx in range(3):
                    last = dve.tensor_scalar(DW[0:96, g, dx, :], eye32[0:96, :], DWC[0:96, g * 3 + dx:g * 3 + dx + 1],
                                             None, ALU.mult)
            last.then_inc(s_dwb, 1)

            taken = [0]

            def chain(i, ins):
                taken[0] += 1
                ins.then_inc(step.sem, 1)
                dve.wait_ge(step.sem, step.at(i, taken[0]))
                carry(dve, i)

            def norm_coefs(i, which, k, before, between=lambda: None):
                chain(i, before)
                for t in range(HALVES):
                    last = dve.bn_aggr(MV[:, t, :], ST[:, t, :, :].rearrange("p c s -> p (c s)"))
                chain(i, last)
                chain(i, dve.tensor_tensor(SQ[:, :], MV[:, :, 0], MV[:, :, 0], ALU.mult))
                dve.tensor_tensor(MV[:, :, 1], MV[:, :, 1], SQ[:, :], ALU.add).then_inc(gn_mv.sem, 1)
                dve.wait_ge(gn_mm.sem, gn_mm.at(i, k))
                carry(dve, i)
                chain(i, dve.tensor_copy(GS[:, :, :], MISC.rearrange("p (t k) -> p t k", t=HALVES)))
                between()
                chain(i, dve.tensor_tensor(SQ[:, :], GS[:, :, 0], GS[:, :, 0], ALU.mult))
                between()
                dve.tensor_tensor(VAR[:, :], GS[:, :, 1], SQ[:, :], ALU.subtract).then_inc(gn_read.sem, 1)
                dve.wait_ge(gn_read.sem, gn_read.at(i, k))
                carry(dve, i)
                chain(i, dve.tensor_scalar(VAR[:, :], VAR[:, :], 0.0, EPS, ALU.max, ALU.add))
                between()
                dve.tensor_scalar(MINUS_HALF[:, :], VAR[:, :], -0.5, None, ALU.mult)
                chain(i, dve.tensor_scalar(HALF_BITS[:, :], VAR[:, :].bitcast(mybir.dt.int32), 1, None,
                                           ALU.logical_shift_right))
                between()
                chain(i, dve.tensor_scalar(RS[:, :].bitcast(mybir.dt.int32), HALF_BITS[:, :], -1.0, RSQRT_GUESS,
                                           ALU.mult, ALU.add))
                between()
                for _ in range(NEWTON):
                    chain(i, dve.tensor_tensor(SQ[:, :], RS[:, :], RS[:, :], ALU.mult))
                    between()
                    chain(i, dve.tensor_tensor(SQ[:, :], SQ[:, :], MINUS_HALF[:, :], ALU.mult))
                    between()
                    chain(i, dve.scalar_tensor_tensor(out=RS[:, :], in0=SQ[:, :], scalar=1.5, in1=RS[:, :],
                                                      op0=ALU.add, op1=ALU.mult))
                    between()
                if which == GN_X:
                    chain(i, dve.tensor_copy(AB[:, which, 0, :], RS[:, :]))
                    between()
                else:
                    chain(i, dve.tensor_tensor(AB[:, which, 0, :], RS[:, :], gn_par[:, which, 0, :], ALU.mult))
                    between()
                chain(i, dve.tensor_tensor(SQ[:, :], GS[:, :, 0], AB[:, which, 0, :], ALU.mult))
                between()
                if which == GN_X:
                    dve.tensor_scalar(AB[:, which, 1, :], SQ[:, :], -1.0, None, ALU.mult).then_inc(gn_ab.sem, 1)
                else:
                    dve.tensor_tensor(AB[:, which, 1, :], gn_par[:, which, 1, :], SQ[:, :], ALU.subtract).then_inc(
                        gn_ab.sem, 1)

            def x_stats(i, k):
                for t in range(HALVES):
                    for c in range(CHUNKS):
                        last = dve.bn_stats(ST[:, t, c, :], X[:, t, c * CHUNK:(c + 1) * CHUNK])
                return last

            def conv_stats(i, first, src):
                for c in range(CHUNKS):
                    for t in range(HALVES):
                        dve.wait_ge(cv_free.sem, cv_free.at(i, first + 2 * c + t + 1))
                        last = dve.bn_stats(ST[:, t, c, :], src[:, t, c * CHUNK:(c + 1) * CHUNK])
                return last

            dve.wait_ge(x_loaded.sem, x_loaded.at(0, CHUNKS))
            norm_coefs(0, GN_X, 0, x_stats(0, 0))
            first_steps = taken[0]

            def image(i, prefetch):
                taken[0] = first_steps
                norm_coefs(i, GN_Q, 1 + GN_Q, conv_stats(i, CV_Q, Q))
                dve.wait_ge(gn_ab.sem, gn_ab.at(i, 1 + GN_Q))
                for t in range(HALVES):
                    last = dve.tensor_scalar(Q[:, t, :], Q[:, t, :], AB[:, GN_Q, 0, t:t + 1], AB[:, GN_Q, 1, t:t + 1],
                                             ALU.mult, ALU.add)
                chain(i, last)
                for t in range(HALVES):
                    last = dve.tensor_reduce(
                        AG[:, t, :].rearrange("p (y x) -> p y x", x=GRID),
                        Q[:, t, :].rearrange("p (y r x s) -> p y x r s", y=GRID, r=CELL, x=GRID), AX.XY, ALU.add)
                chain(i, last)
                for h in range(HALF_HEADS):
                    rows = slice(HEAD_DIM * h, HEAD_DIM * (h + 1))
                    last = dve.tensor_scalar(M2[rows, :, AGENTS * h:AGENTS * (h + 1)], AG[rows, :, :],
                                             SCALE / CELL ** 2, None, ALU.mult)
                last.then_inc(m2_ready.sem, 1)

                norm_coefs(i, GN_K, 1 + GN_K, conv_stats(i, CV_K, KP))
                dve.wait_ge(gn_ab.sem, gn_ab.at(i, 1 + GN_K))
                for t in range(HALVES):
                    last = dve.tensor_scalar(M1[:, t, :], M2[:, t, :], AB[:, GN_K, 0, t:t + 1], None, ALU.mult)
                last.then_inc(m1_ready.sem, 1)

                def add_agent_bias(p, c):
                    n = CHUNKS * p + c
                    dve.wait_ge(sc_full.sem, sc_full.at(i, n + 1))
                    carry(dve, i)
                    dve.wait_ge(b1_loaded[n % 4].sem, b1_loaded[n % 4].at(i, n // 4 + 1))
                    carry(dve, i)
                    if c == 0 and p >= 2:
                        dve.wait_ge(pt_read.sem, pt_read.at(i, CHUNKS * (p - 1)))
                        carry(dve, i)
                    dve.tensor_tensor_reduce(
                        T1[0:PAIR, p % 2, c * CHUNK:(c + 1) * CHUNK], SC[n % 2][0:PAIR, 0:CHUNK],
                        B1[0:PAIR, n % 4, :], 1.0, -3.0e38, ALU.add, ALU.max,
                        MX[0:PAIR, c:c + 1]).then_inc(sc_free.sem, 1)

                def agent_maximum(p):
                    dve.wait_ge(sc_free.sem, sc_free.at(i, CHUNKS * (p + 1)))
                    chain(i, dve.tensor_reduce(MAX[0:PAIR, p:p + 1], MX[0:PAIR, :], AX.X, ALU.max))
                    dve.tensor_scalar(NM[0:PAIR, p:p + 1], MAX[0:PAIR, p:p + 1], -1.0, None, ALU.mult).then_inc(
                        nmx.sem, 1)

                def agent_scores(p):
                    for c in range(CHUNKS):
                        add_agent_bias(p, c)
                    agent_maximum(p)

                def norm_among_scores(which, k, before, p):
                    left = list(range(CHUNKS))

                    def next_chunk():
                        if left:
                            add_agent_bias(p, left.pop(0))

                    norm_coefs(i, which, k, before, next_chunk)
                    agent_maximum(p)

                def agent_values(p):
                    dve.wait_ge(avt.sem, avt.at(i, p + 1))
                    chain(i, dve.tensor_tensor(INV[0:PAIR, p:p + 1], SUMS[0:PAIR, p, 0:1], SUMS[0:PAIR, p, 1:2], ALU.add))
                    chain(i, dve.reciprocal(INV[0:PAIR, p:p + 1], INV[0:PAIR, p:p + 1]))
                    at = 2 * HEAD_DIM * (p % 2)
                    dve.scalar_tensor_tensor(out=AGV[0:PAIR, p, :], in0=AVT[:, at:at + 2 * HEAD_DIM],
                                             scalar=INV[0:PAIR, p:p + 1], in1=pair_mask[0:PAIR, :],
                                             op0=ALU.mult, op1=ALU.mult).then_inc(agv.sem, 1)

                def query_scores(c):
                    for s in range(SUBS):
                        n = PAIRS * CHUNKS + SUBS * c + s
                        dve.wait_ge(sc_full.sem, sc_full.at(i, n + 1))
                        if s == 0:
                            if c == 0:
                                dve.wait_ge(pt_read.sem, pt_read.at(i, 3 * CHUNKS))
                            if c >= 2:
                                dve.wait_ge(tr_full.sem, tr_full.at(i, TR_P2 + PAIRS * (c - 1)))
                            dve.wait_ge(b2_loaded[c % 2].sem, b2_loaded[c % 2].at(i, c // 2 + 1))
                        m = slice(s * ALL_AGENTS, (s + 1) * ALL_AGENTS)
                        last = dve.tensor_tensor(T2[0:SUB, c % 2, m], SC[n % 2][0:SUB, 0:ALL_AGENTS],
                                                 B2[0:SUB, c % 2, m], ALU.add)
                        last.then_inc(sc_free.sem, 1)
                    dve.wait_ge(sc_free.sem, sc_free.at(i, PAIRS * CHUNKS + SUBS * (c + 1)))
                    dve.tensor_reduce(QM[0:SUB, c % 2, :], T2[0:SUB, c % 2, :].rearrange("p (m a) -> p m a", a=AGENTS),
                                      AX.X, ALU.max).then_inc(q_max.sem, 1)

                def query_sums(c):
                    dve.wait_ge(q_exp.sem, q_exp.at(i, c + 1))
                    chain(i, dve.tensor_reduce(QS[0:SUB, c % 2, :],
                                               T2[0:SUB, c % 2, :].rearrange("p (m a) -> p m a", a=AGENTS),
                                               AX.X, ALU.add))
                    dve.reciprocal(QS[0:SUB, c % 2, :], QS[0:SUB, c % 2, :]).then_inc(q_sum.sem, 1)

                norm_among_scores(GN_V, 1 + GN_V, conv_stats(i, CV_V, V_IN), 0)
                agent_scores(1)
                agent_scores(2)
                agent_values(0)
                if prefetch:
                    dve.wait_ge(x_loaded.sem, x_loaded.at(i + 1, CHUNKS))
                    norm_among_scores(GN_X, 1 + GN_X, x_stats(i, 1 + GN_X), 3)
                else:
                    agent_scores(3)
                agent_values(1)
                query_scores(0)
                agent_values(2)
                query_scores(1)
                agent_values(3)
                query_sums(0)
                for c in range(CHUNKS):
                    if c + 1 < CHUNKS:
                        query_sums(c + 1)
                    if c + 2 < CHUNKS:
                        query_scores(c + 2)
                    if c:
                        for t in range(HALVES):
                            dve.wait_ge(cv_free.sem, cv_free.at(i, CV_P + 2 * (c - 1) + t + 1))
                            dve.bn_stats(ST[:, t, c - 1, :], KP[:, t, (c - 1) * CHUNK:c * CHUNK])
                for t in range(HALVES):
                    dve.wait_ge(cv_free.sem, cv_free.at(i, CV_P + 2 * (CHUNKS - 1) + t + 1))
                    last = dve.bn_stats(ST[:, t, CHUNKS - 1, :], KP[:, t, (CHUNKS - 1) * CHUNK:])
                norm_coefs(i, GN_P, 1 + (GN_P if prefetch else GN_X), last)
                if prefetch:
                    assert taken[0] - first_steps == STEPS, taken[0] - first_steps

            if B > 1:
                with dve.Fori(0, B - 1) as i:
                    image(i, True)
            image(B - 1, False)

        @block.tensor
        def _(pe):
            for s, credit in ((dw_done.sem, 2), (pt_read.sem, 2)):
                pe.sem_inc(s, credit)
            pe.wait_ge(s_const, 16 * 8)
            for n in range(PAIRS * CHUNKS + TILES):
                if n >= 2:
                    pe.wait_ge(s_bev, n - 1)
                if n < PAIRS * CHUNKS:
                    p, c = n // CHUNKS, n % CHUNKS
                    for half, k in ((0, BASIS_A), (1, BASIS_B)):
                        last = pe.matmul(SC[n % 2][0:PAIR, 0:CHUNK], KP[0:k, half, PAIR * p:PAIR * (p + 1)],
                                         Q[0:k, half, c * CHUNK:(c + 1) * CHUNK], start=(half == 0), stop=(half == 1))
                else:
                    u = n - PAIRS * CHUNKS
                    for half, k in ((0, BASIS_A), (1, BASIS_B)):
                        last = pe.matmul(SC[n % 2][0:SUB, 0:ALL_AGENTS], Q[0:k, half, SUB * u:SUB * (u + 1)],
                                         KP[0:k, half, ALL_AGENTS:2 * ALL_AGENTS], start=(half == 0), stop=(half == 1))
                last.then_inc(s_bmm, 1)

            def group_stats(i, k):
                pe.wait_ge(gn_mv.sem, gn_mv.at(i, k))
                pe.matmul(MISC, group_mean, MV[:, :, :].rearrange("p t k -> p (t k)"), start=True, stop=True).then_inc(
                    gn_mm.sem, 1)

            pe.wait_ge(s_dwb, 1)
            group_stats(0, 0)

            def conv(i, first, j, c, rhs):
                for t in range(HALVES):
                    n = first + 2 * c + t
                    pe.wait_ge(cv_free.sem, cv_free.at(i, n + 1 - 2))
                    for k in range(HALVES):
                        last = pe.matmul(CV[n % 2][:, 0:CHUNK], WT[:, j, k, t * P:(t + 1) * P], rhs(c, k),
                                         start=(k == 0), stop=(k == HALVES - 1))
                    last.then_inc(cv_full.sem, 1)

            def x_in(c, k):
                return X[:, k, c * CHUNK:(c + 1) * CHUNK]

            def first_convs(i):
                pe.wait_ge(x_norm.sem, x_norm.at(i, HALVES))
                for c in range(2):
                    conv(i, CV_Q, 0, c, x_in)

            first_convs(0)

            def image(i, prefetch):
                for c in range(2, CHUNKS):
                    conv(i, CV_Q, 0, c, x_in)
                for c in range(CHUNKS):
                    conv(i, CV_K, 1, c, x_in)
                    if c == 1:
                        group_stats(i, 1 + GN_Q)
                for c in range(CHUNKS):
                    conv(i, CV_V, 2, c, x_in)
                    if c == 2:
                        group_stats(i, 1 + GN_K)

                def turn_v(t):
                    pe.wait_ge(v_norm.sem, v_norm.at(i, t + 1))
                    for u in range(CHUNKS):
                        n = TR_VT[t] + u
                        pe.wait_ge(tr_free.sem, tr_free.at(i, n + 1 - 2))
                        for s in range(SUBS):
                            v = V_IN[:, t, SUB * (SUBS * u + s):SUB * (SUBS * u + s + 1)]
                            last = pe.transpose(TR[n % 2][0:SUB, s * P:(s + 1) * P], v, ident)
                        last.then_inc(tr_full.sem, 1)

                def agent_scores(p):
                    for c in range(CHUNKS):
                        n = CHUNKS * p + c
                        pe.wait_ge(sc_free.sem, sc_free.at(i, n + 1 - 2))
                        pe.matmul(SC[n % 2][0:PAIR, 0:CHUNK], M1[:, p // 2, PAIR * (p % 2):PAIR * (p % 2 + 1)],
                                  KP[:, p // 2, c * CHUNK:(c + 1) * CHUNK], start=True, stop=True).then_inc(sc_full.sem, 1)
                        if n == 1:
                            group_stats(i, 1 + GN_V)

                def agent_sum(p, c):
                    pe.wait_ge(tr_free.sem, tr_free.at(i, TR_PT[p] + c + 1))
                    for s in range(SUBS):
                        u = SUBS * c + s
                        last = pe.matmul(YA[0][:, 0:PAIR], VT[:, u, :],
                                         PT[0:SUB, (CHUNKS * p + c) % 2, PAIR * s:PAIR * (s + 1)],
                                         start=(u == 0), stop=(u == TILES - 1))
                    last.then_inc(pt_read.sem, 1)

                def agent_out(p):
                    if p:
                        pe.wait_ge(avs.sem, avs.at(i, p))
                    for c in range(CHUNKS):
                        if c in PARTS:
                            pe.wait_ge(exp1.sem, exp1.at(i, 2 * p + 1 + PARTS.index(c)))
                        n = TR_PT[p] + c
                        pe.wait_ge(tr_free.sem, tr_free.at(i, n + 1 - 2))
                        for s in range(SUBS):
                            u = SUBS * c + s
                            last = pe.transpose(TR[n % 2][0:SUB, PAIR * s:PAIR * (s + 1)],
                                                T1[0:PAIR, p % 2, SUB * u:SUB * (u + 1)], ident[0:PAIR, 0:PAIR])
                        last.then_inc(tr_full.sem, 1)
                        if c:
                            agent_sum(p, c - 1)
                    agent_sum(p, CHUNKS - 1)

                def turn_agent_v(p):
                    pe.wait_ge(avs.sem, avs.at(i, p + 1))
                    if p:
                        pe.wait_ge(agv.sem, agv.at(i, p))
                    pe.transpose(AVT, AVS[:, :], ident).then_inc(avt.sem, 1)

                def query_scores(c):
                    for s in range(SUBS):
                        u = SUBS * c + s
                        n = PAIRS * CHUNKS + u
                        pe.wait_ge(sc_free.sem, sc_free.at(i, n + 1 - 2))
                        for t in range(HALVES):
                            last = pe.matmul(SC[n % 2][0:SUB, HALF_AGENTS * t:HALF_AGENTS * (t + 1)],
                                             Q[:, t, SUB * u:SUB * (u + 1)], M2[:, t, :], start=True, stop=True)
                        last.then_inc(sc_full.sem, 1)

                pe.wait_ge(m1_ready.sem, m1_ready.at(i, 1))
                agent_scores(0)
                agent_scores(1)
                turn_v(0)
                agent_out(0)
                agent_scores(2)
                turn_agent_v(0)
                agent_out(1)
                turn_v(1)
                if prefetch:
                    pe.wait_ge(agv.sem, agv.at(i, 1))
                    group_stats(i, 1 + GN_X)
                agent_scores(3)
                if prefetch:
                    pe.wait_ge(gn_read.sem, gn_read.at(i, 1 + GN_X))
                turn_agent_v(1)
                agent_out(2)
                query_scores(0)
                turn_agent_v(2)
                agent_out(3)
                query_scores(1)
                turn_agent_v(3)

                def depthwise(c, t):
                    if c == 0 and t == 1:
                        pe.wait_ge(agv.sem, agv.at(i, PAIRS))
                    pe.wait_ge(vg_loaded.sem, vg_loaded.at(i, c + 1))
                    pe.wait_ge(y_free.sem, y_free.at(i, 2 * c + t + 1 - 2))
                    for dx, to, of in ((1, 0, 0), (0, 1, 0), (2, 0, 1)):
                        w = W if dx == 1 else W - 1
                        for q in range(4):
                            out = YA[t][32 * q:32 * (q + 1), 0:CHUNK].rearrange("p (h w) -> p h w", w=W)[:, :, to:to + w]
                            rows = VG[:, t, q, :].rearrange("p (h w) -> p h w", w=W)[:, :, of:of + w]
                            last = pe.matmul(out, DW[:, 4 * t + q, dx, :], rows, start=(dx == 1), stop=False,
                                             skip_group_check=True)
                    last.then_inc(dw_done.sem, 1)

                def turn_query(c):
                    pe.wait_ge(q_mul.sem, q_mul.at(i, c + 1))
                    for p in range(PAIRS):
                        n = TR_P2 + PAIRS * c + p
                        pe.wait_ge(tr_free.sem, tr_free.at(i, n + 1 - 2))
                        for s in range(SUBS):
                            m = s * ALL_AGENTS + PAIR * p
                            last = pe.transpose(TR[n % 2][0:PAIR, SUB * s:SUB * (s + 1)],
                                                T2[0:SUB, c % 2, m:m + PAIR], ident[0:SUB, 0:SUB])
                        last.then_inc(tr_full.sem, 1)

                def attend(c):
                    for t in range(HALVES):
                        pe.wait_ge(tr_free.sem, tr_free.at(i, TR_P2 + PAIRS * c + 2 * t + 2))
                        for g in range(2):
                            last = pe.matmul(YA[t][64 * g:64 * (g + 1), 0:CHUNK], AGV[:, 2 * t + g, :],
                                             P2[:, c % 2, 2 * t + g, :], start=False, stop=True, skip_group_check=True)
                        last.then_inc(y_full.sem, 1)

                def project(c):
                    pe.wait_ge(y_free.sem, y_free.at(i, 2 * (c + 1)))
                    conv(i, CV_P, 3, c, lambda c, k: Y[:, c % 2, k, :])

                for c in range(CHUNKS):
                    for t in range(HALVES):
                        depthwise(c, t)
                    turn_query(c)
                    attend(c)
                    if c + 2 < CHUNKS:
                        query_scores(c + 2)
                    if c:
                        project(c - 1)
                project(CHUNKS - 1)
                if prefetch:
                    first_convs(i + 1)
                group_stats(i, 1 + (GN_P if prefetch else GN_X))

            if B > 1:
                with pe.Fori(0, B - 1) as i:
                    image(i, True)
            image(B - 1, False)


TR_VT = [0, CHUNKS + 2 * CHUNKS]
TR_PT = [CHUNKS, 2 * CHUNKS, 4 * CHUNKS, 5 * CHUNKS]
TR_P2 = 6 * CHUNKS
STEPS = 5 * (7 + 3 + 3 * NEWTON) + 2 + PAIRS * 3 + CHUNKS


def layouts(x, p):
    B = x.shape[0]
    at = lambda n: np.asarray(p[f"L0_conv_{n}"])
    by_half = lambda v: v.reshape(HALVES, P).T
    weights = np.stack([at(f"{n}_w").T.reshape(HALVES, P, C) for n in "qkvp"])
    params = [by_half(at(f"{n}_g{k}")) for n in "qkv" for k in "wb"]
    params += [np.zeros((P, 2 * HALVES), np.float32)]
    params += [by_half(at(f"p_g{k}")) for k in "wb"] + [by_half(at("dwc_b"))]
    taps = at("dwc_w").reshape(PATCHES, HEAD_DIM, 3, 3).transpose(2, 1, 0, 3)
    coefs = np.concatenate([
        np.concatenate([at("an_bias").reshape(ALL_AGENTS, GRID * GRID).T, at("ah_bias").reshape(ALL_AGENTS, H).T,
                        at("aw_bias").reshape(ALL_AGENTS, W).T]),
        np.concatenate([at("na_bias").reshape(ALL_AGENTS, GRID * GRID).T,
                        at("ha_bias").reshape(HEADS, H, AGENTS).transpose(1, 0, 2).reshape(H, ALL_AGENTS),
                        at("wa_bias").reshape(HEADS, W, AGENTS).transpose(1, 0, 2).reshape(W, ALL_AGENTS)])], axis=1)
    where = (np.arange(H) + 0.5) / CELL - 0.5
    line = np.maximum(0, 1 - np.abs(where[None, :] - np.arange(GRID)[:, None]))
    line /= line.sum(0)
    grid = np.einsum("iy,jx->ijyx", line, line).reshape(GRID * GRID, N)
    ys = np.repeat(np.eye(H), W, axis=1)
    xs = np.tile(np.eye(W), (1, H))
    same_group = np.kron(np.eye(P // GROUP), np.ones((GROUP, GROUP))) / GROUP
    heads = np.zeros((P, 2 * HEAD_DIM))
    heads[:PAIR] = np.kron(np.eye(2), np.ones((AGENTS, HEAD_DIM)))
    constants = np.concatenate([np.eye(P), same_group, np.tile(np.eye(HEAD_DIM), (P // HEAD_DIM, 1)), heads], axis=1)
    return {
        "x": np.asarray(x).reshape(B, C, N),
        "weights": np.ascontiguousarray(weights.transpose(2, 0, 1, 3).reshape(P, 4 * HALVES * C)),
        "params": np.ascontiguousarray(np.concatenate(params, axis=1)),
        "taps": np.ascontiguousarray(taps.reshape(3 * HEAD_DIM, PATCHES * 3)),
        "bias_coefs": np.ascontiguousarray(coefs),
        "basis": np.concatenate([grid, ys, xs]).astype(np.float32),
        "constants": constants.astype(np.float32),
    }


def kernel(x, **params):
    import concourse.bacc as bacc
    from concourse.bass_utils import run_bass_kernel_spmd

    B = x.shape[0]
    arrays = layouts(x, params)
    nc = bacc.Bacc("TRN2", target_bir_lowering=False, num_devices=1)
    dram = {n: nc.dram_tensor(n, v.shape, F32, kind="ExternalInput").ap() for n, v in arrays.items()}
    dram["out"] = nc.dram_tensor("out", (B, C, N), F32, kind="ExternalOutput").ap()
    attention_block(nc, B, dram)
    r = run_bass_kernel_spmd(nc, [arrays], core_ids=[0])
    return r.results[0]["out"].reshape(B, C, H, W)
```

```python
from contextlib import ExitStack

import numpy as np

import concourse.bass as bass
from concourse import mybir

F32 = mybir.dt.float32
ALU = mybir.AluOpType
ACT = mybir.ActivationFunctionType
AX = mybir.AxisListType

P = 128
C = 256
HALVES = C // P
H = W = 56
N = H * W
HEADS = 8
HEAD_DIM = C // HEADS
AGENTS = 49
GRID = 7
CELL = H // GRID
PAIRS = HEADS // 2
PAIR = 2 * AGENTS
HALF_HEADS = HEADS // HALVES
HALF_AGENTS = HALF_HEADS * AGENTS
ALL_AGENTS = HEADS * AGENTS
GROUP = C // 32
SCALE = HEAD_DIM ** -0.5
EPS = 1e-5
RSQRT_GUESS = float(0x5F3759DF)
NEWTON = 3

ROWS = 8
CHUNK = ROWS * W
CHUNKS = H // ROWS
SUB = 112
SUBS = CHUNK // SUB
TILES = N // SUB
PATCHES = C // HEAD_DIM
WINDOW = 22
WINDOWS = -(-H // WINDOW)
BASIS = GRID * GRID + W + WINDOW
BLOCK = SUBS * HALF_AGENTS
BLOCKS = HALVES * CHUNKS
BANK = BLOCK // 2
DVE_SHIFTS = 4

GN_Q, GN_K, GN_V, GN_X, GN_P = range(5)
CV_PER = 2 * CHUNKS
CV_Q, CV_K, CV_V, CV_P = (j * CV_PER for j in range(4))


class Count:

    def __init__(self, sem, per, credit=0, unit=1):
        self.sem, self.per, self.credit, self.unit = sem, per, credit, unit

    def at(self, i, k):
        return i * (self.per * self.unit) + (k * self.unit + self.credit)


def attention_block(nc, B, a):
    ctx = ExitStack()
    with ctx:
        def sb(name, shape, dt=F32):
            return ctx.enter_context(nc.sbuf_tensor("sb_" + name, shape, dt))

        def sem(name):
            return ctx.enter_context(nc.semaphore(name))

        X = sb("x_norm", [P, HALVES, N])
        Q = sb("q", [P, HALVES, N])
        KP = sb("k_then_projection", [P, HALVES, N])
        V = sb("v_padded", [P, HALVES, (H + 2) * W])
        A = sb("scores_by_position", [P, HALVES, TILES * HALF_AGENTS])
        VT = sb("v_by_position", [P, TILES, 2, 2 * HEAD_DIM + 1])
        VG = sb("v_three_rows", [P, 2, PATCHES // 2, CHUNK])
        BIAS = sb("bias", [P, 4, BLOCK])
        WT = sb("weights", [P, 4, HALVES, C])
        DW = sb("depthwise_diagonals", [P, PATCHES, 3, HEAD_DIM])
        CONST = sb("constants", [P, 2 * P + HEAD_DIM + 2 * HEAD_DIM])
        PAR = sb("params", [P, 5 * 2 * HALVES + HALVES])
        DWC = sb("depthwise_taps", [P, PATCHES * 3])
        M1 = sb("agents_for_k", [P, HALVES, HALF_AGENTS])
        M2 = sb("agents_for_q", [P, HALVES, HALF_AGENTS])
        AG = sb("pooled_q", [P, HALVES, AGENTS])
        AGV = sb("agent_v", [P, PAIRS, 2 * HEAD_DIM])
        ONES = sb("ones", [P, SUB])
        CHUNK_MAX = sb("chunk_maxima", [P, SUBS * HALF_AGENTS])
        TILE_MAX = sb("tile_maxima", [P, HALF_AGENTS])
        MAX = sb("agent_maxima", [P, 2])
        MAX_DIAG = AVS = TILE_MAX[:, :].rearrange("p (g a) -> p g a", g=2)
        MAX_ROW = sb("agent_maxima_row", [P, HALVES, HALF_AGENTS])
        ST = sb("chunk_stats", [P, HALVES, CHUNKS, 6])
        STX = sb("chunk_stats_of_x", [P, HALVES, CHUNKS, 6])
        MV = sb("channel_stats", [P, HALVES, 2])
        SQ = sb("squares", [P, HALVES])
        GS = sb("group_stats", [P, HALVES, 2])
        VAR = sb("group_variance", [P, HALVES])
        RS = sb("group_rsqrt", [P, HALVES])
        HALF_BITS = sb("halved_bits", [P, HALVES], mybir.dt.int32)
        MINUS_HALF = sb("minus_half_variance", [P, HALVES])
        AB = sb("scale_and_shift", [P, 5, 2, HALVES])
        INV = sb("agent_sums_inverse", [P, PAIRS])
        QM = sb("query_maxima", [P, 2, SUBS * HEADS])
        QS = sb("query_sums", [P, 2, SUBS * HEADS])

        A_IN = A[0:SUB, :, :].rearrange("p t (u a) -> p t u a", a=HALF_AGENTS)
        T2 = A[:, 0, 0:2 * SUBS * ALL_AGENTS].rearrange("p (s m) -> p s m", s=2)
        Y = A[:, 0, 2 * SUBS * ALL_AGENTS:2 * SUBS * ALL_AGENTS + 4 * CHUNK].rearrange("p (s t n) -> p s t n", s=2, t=HALVES)
        P2 = A[:, 1, 0:2 * PAIRS * CHUNK].rearrange("p (s g n) -> p s g n", s=2, g=PAIRS)
        XR = A[:, 1, 2 * PAIRS * CHUNK:2 * PAIRS * CHUNK + 4 * CHUNK].rearrange("p (s t n) -> p s t n", s=2, t=HALVES)
        V_IN = V[:, :, W:W + N]
        ident = CONST[:, 0:P]
        group_mean = CONST[:, P:2 * P]
        eye32 = CONST[:, 2 * P:2 * P + HEAD_DIM]
        pair_mask = CONST[:, 2 * P + HEAD_DIM:2 * P + 3 * HEAD_DIM]
        gn_par = PAR[:, 0:20].rearrange("p (n k t) -> p n k t", n=5, k=2)
        dwc_b = PAR[:, 20:22]

        CV = [ctx.enter_context(nc.psum_tensor(f"conv{j}", [P, 512], F32)) for j in range(2)]
        SC = [ctx.enter_context(nc.psum_tensor(f"score{j}", [P, 512], F32)) for j in range(2)]
        TR = [ctx.enter_context(nc.psum_tensor(f"turn{j}", [P, 512], F32)) for j in range(2)]
        YA = [ctx.enter_context(nc.psum_tensor(f"sum{j}", [P, 512], F32)) for j in range(2)]
        GROUP_SUMS = YA[1][:, 256:256 + 2 * HALVES]
        GROUP_SUMS_X = CV[0][:, 0:2 * HALVES]
        V_ROWS = 2 * HEAD_DIM + 1
        AV = [bank[0:V_ROWS, 0:PAIR] for bank in YA + CV]
        AV_TURNED = [bank[0:PAIR, 0:V_ROWS] for bank in YA + CV]
        MAX_TURNED = CV[0][0:PAIR, 0:2 * SUB]
        MAX_SPREAD = CV[1][0:SUB, 0:HALF_AGENTS]

        b1_dram = nc.dram_tensor("agent_bias_table", [CHUNKS, SUB, HALVES * BLOCK], F32, kind="Internal").ap()
        b2_dram = nc.dram_tensor("query_bias_table", [CHUNKS, SUB, SUBS * ALL_AGENTS], F32, kind="Internal").ap()
        v_dram = nc.dram_tensor("v_rows", [HEAD_DIM, PATCHES, (H + 2) * W], F32, kind="Internal").ap()
        x_v = a["x"].rearrange("b (t p) n -> b p t n", p=P)
        out_v = a["out"].rearrange("b (t p) n -> b p t n", p=P)

        waited = sem("waited")
        s_const = sem("consts_loaded")
        s_zero = sem("zeroed")
        s_dwb = sem("depthwise_built")
        s_bmm = sem("bias_matmul")
        s_bev = sem("bias_copied")
        s_table_out = [sem(f"bias_stored{j}") for j in range(2)]
        x_loaded = Count(sem("x_loaded"), CHUNKS, unit=16)
        gn_mv = Count(sem("gn_channel_stats_ready"), 5, 1)
        gn_mm = Count(sem("gn_group_stats_ready"), 5, 1)
        gn_read = Count(sem("gn_group_stats_read"), 5, 1)
        gn_ab = Count(sem("gn_scale_shift_ready"), 5, 1)
        x_norm = Count(sem("x_normalised"), HALVES, 0)
        v_norm = Count(sem("v_normalised"), HALVES, 0)
        cv_full = Count(sem("conv_bank_full"), 4 * CV_PER)
        cv_free = Count(sem("conv_bank_read"), 4 * CV_PER, 2)
        sc_full = Count(sem("score_bank_full"), 2 * BLOCKS + TILES)
        sc_free = Count(sem("score_bank_read"), 2 * BLOCKS + TILES, 2)
        tr_full = Count(sem("turn_bank_full"), 2 * CHUNKS + PAIRS * CHUNKS)
        tr_free = Count(sem("turn_bank_read"), 2 * CHUNKS + PAIRS * CHUNKS, 2)
        m2_ready = Count(sem("agents_for_q_ready"), 1)
        m1_ready = Count(sem("agents_for_k_ready"), 1)
        b1_loaded = [Count(sem(f"agent_bias_loaded{j}"), (BLOCKS + 3 - j) // 4, unit=16) for j in range(4)]
        b2_loaded = [Count(sem(f"query_bias_loaded{j}"), (CHUNKS + 1 - j) // 2, unit=16) for j in range(2)]
        tile_max = Count(sem("tile_maxima_ready"), HALVES)
        max_turned = Count(sem("maxima_turned"), HALVES)
        max_diag = Count(sem("maxima_diagonal_ready"), HALVES)
        max_spread = Count(sem("maxima_spread"), HALVES)
        max_row = Count(sem("maxima_row_ready"), HALVES)
        biased = Count(sem("agent_scores_biased"), CHUNKS)
        shifted = [Count(sem(f"agent_scores_shifted{j}"), n) for j, n in
                   enumerate((CHUNKS, DVE_SHIFTS, CHUNKS - DVE_SHIFTS))]
        exp1 = Count(sem("agent_weights_ready"), BLOCKS)
        av_done = Count(sem("agent_v_summed"), HALVES)
        avs = Count(sem("agent_v_copied"), PAIRS)
        avt = Count(sem("agent_v_turned"), PAIRS)
        agv = Count(sem("agent_v_ready"), PAIRS)
        q_max = Count(sem("query_maxima_ready"), CHUNKS)
        q_sub = Count(sem("query_scores_shifted"), CHUNKS)
        q_exp = Count(sem("query_weights_ready"), CHUNKS)
        q_sum = Count(sem("query_sums_ready"), CHUNKS)
        q_mul = Count(sem("query_weights_scaled"), CHUNKS)
        dw_done = Count(sem("depthwise_done"), 2 * CHUNKS, 2)
        v_stored = Count(sem("v_stored"), 1, unit=16 * 4)
        vg_loaded = Count(sem("v_rows_loaded"), CHUNKS, unit=16 * 3)
        y_full = Count(sem("attention_out_summed"), 2 * CHUNKS)
        y_free = Count(sem("attention_out_copied"), 2 * CHUNKS, 2)
        xr_loaded = [Count(sem(f"x_again_loaded{j}"), (CHUNKS + 1 - j) // 2, unit=16) for j in range(2)]
        p_affine = Count(sem("projection_normalised"), 2 * CHUNKS)
        res_done = Count(sem("residual_added"), CHUNKS, 1)
        stored = [Count(sem(f"out_stored{c}"), 1, 1, unit=16) for c in range(CHUNKS)]
        step = Count(sem("vector_step"), STEPS)

        def query_slots(c):
            j = 2 - 2 * (c % 2)
            return BIAS[0:SUB, j:j + 2, :].rearrange("p j m -> p (j m)")

        def carry(eng, i):
            if not isinstance(i, int):
                eng.sem_inc(waited, 1)

        tables_stored = [(s_table_out[j], 16 * CHUNKS) for j in range(2)]

        block = ctx.enter_context(nc.Block())

        @block.sync
        def _(sp):
            for dst, src in ((WT[:, :, :, :], a["weights"].rearrange("p (j k o) -> p j k o", j=4, k=HALVES)),
                             (CONST[:, :], a["constants"]), (PAR[:, :], a["params"]),
                             (DWC[0:96, :], a["taps"]),
                             (Q[0:BASIS, 0, :], a["basis"]),
                             (KP[0:BASIS, 0, 0:WINDOWS * 2 * ALL_AGENTS], a["bias_coefs"])):
                sp.dma_start(dst, src).then_inc(s_const, 16)

            def load_x(i, c):
                n = slice(c * CHUNK, (c + 1) * CHUNK)
                sp.dma_start(X[:, :, n], x_v[i][:, :, n]).then_inc(x_loaded.sem, 16)

            for c in range(CHUNKS):
                load_x(0, c)
            sp.wait_ge(s_zero, ZEROED)
            for c in range(2 * CHUNKS):
                sp.wait_ge(s_bev, SUBS * (c + 1))
                sp.dma_start(b1_dram[c] if c < CHUNKS else b2_dram[c - CHUNKS],
                             A[0:SUB, c % 2, 0:SUBS * ALL_AGENTS]).then_inc(s_table_out[c % 2], 16)
            for s, n in tables_stored:
                sp.wait_ge(s, n)

            def image(i, prefetch):
                def store_v():
                    sp.wait_ge(v_norm.sem, v_norm.at(i, HALVES))
                    carry(sp, i)
                    for q in range(4):
                        sp.dma_start(v_dram.rearrange("p (t q) n -> q p t n", q=4)[q],
                                     V[HEAD_DIM * q:HEAD_DIM * (q + 1), :, :]).then_inc(v_stored.sem, 16)

                def rows(c):
                    if c == 0:
                        sp.wait_ge(v_stored.sem, v_stored.at(i, 1))
                        carry(sp, i)
                    sp.wait_ge(dw_done.sem, dw_done.at(i, 2 * c))
                    carry(sp, i)
                    for s in range(3):
                        at = (ROWS * c + s) * W
                        sp.dma_start(VG[HEAD_DIM * s:HEAD_DIM * (s + 1), :, :, :].rearrange("p t q n -> p (t q) n"),
                                     v_dram[:, :, at:at + CHUNK]).then_inc(vg_loaded.sem, 16)

                for n in range(BLOCKS):
                    t, c = n // CHUNKS, n % CHUNKS
                    if 4 <= n < 4 + CHUNKS:
                        sp.wait_ge(biased.sem, biased.at(i, n - 3))
                    else:
                        sp.wait_ge(sc_free.sem, sc_free.at(i, 2 * (n - 3) if n >= 4 else 0))
                    carry(sp, i)
                    sp.dma_start(BIAS[0:SUB, n % 4, :], b1_dram[c][:, t * BLOCK:(t + 1) * BLOCK]).then_inc(
                        b1_loaded[n % 4].sem, 16)
                    if prefetch and n == 3:
                        for x_chunk in range(CHUNKS):
                            sp.wait_ge(cv_full.sem, cv_full.at(i, CV_V + 2 * (x_chunk + 1)))
                            carry(sp, i)
                            load_x(i + 1, x_chunk)

                def query_bias(c):
                    sp.wait_ge(sc_free.sem, sc_free.at(i, (2 * (BLOCKS - 2 * (1 - c)) if c < 2 else
                                                           2 * BLOCKS + SUBS * (c - 1))))
                    carry(sp, i)
                    sp.dma_start(query_slots(c), b2_dram[c]).then_inc(b2_loaded[c % 2].sem, 16)

                store_v()
                query_bias(0)
                rows(0)
                query_bias(1)
                for c in range(2, CHUNKS):
                    query_bias(c)
                    rows(c - 1)
                rows(CHUNKS - 1)
                for c in range(CHUNKS):
                    sp.wait_ge(res_done.sem, res_done.at(i, c + 1 - 2 if c >= 2 else 0))
                    carry(sp, i)
                    sp.dma_start(XR[:, c % 2, :, :], x_v[i][:, :, c * CHUNK:(c + 1) * CHUNK]).then_inc(
                        xr_loaded[c % 2].sem, 16)
                    if c >= 1:
                        store(i, c - 1)
                store(i, CHUNKS - 1)

            def store(i, c):
                sp.wait_ge(res_done.sem, res_done.at(i, c + 1))
                carry(sp, i)
                sp.dma_start(out_v[i][:, :, c * CHUNK:(c + 1) * CHUNK], KP[:, :, c * CHUNK:(c + 1) * CHUNK]).then_inc(
                    stored[c].sem, 16)

            if B > 1:
                with sp.Fori(0, B - 1) as i:
                    image(i, True)
            image(B - 1, False)
            for c in range(CHUNKS):
                sp.wait_ge(stored[c].sem, stored[c].at(B - 1, 1))

        @block.gpsimd
        def _(pool):
            for c in range(CHUNKS):
                pool.sem_inc(stored[c].sem, 1)

            def norm_x(i, n, t):
                if t == 0:
                    pool.wait_ge(gn_ab.sem, gn_ab.at(i, n))
                    carry(pool, i)
                pool.tensor_scalar(X[:, t, :], X[:, t, :], AB[:, GN_X, 0, t:t + 1], AB[:, GN_X, 1, t:t + 1],
                                   ALU.mult, ALU.add).then_inc(x_norm.sem, 1)

            for t in range(HALVES):
                norm_x(0, 0, t)

            def image(i, prefetch):
                def shift_agents(t, chunks):
                    pool.wait_ge(max_row.sem, max_row.at(i, t + 1))
                    for c in chunks:
                        scores = A_IN[:, t, SUBS * c:SUBS * (c + 1), :]
                        pool.tensor_tensor(scores, scores, MAX_ROW[0:SUB, t:t + 1, :].broadcast_to([SUB, SUBS, HALF_AGENTS]),
                                           ALU.subtract).then_inc(shifted[2 * t].sem, 1)

                for c in range(CHUNKS):
                    pool.wait_ge(sc_free.sem, sc_free.at(i, 2 * (c + 1)))
                    carry(pool, i)
                    pool.wait_ge(b1_loaded[c % 4].sem, b1_loaded[c % 4].at(i, c // 4 + 1))
                    scores = A[0:SUB, 0, c * BLOCK:(c + 1) * BLOCK]
                    pool.tensor_tensor(scores, scores, BIAS[0:SUB, c % 4, :], ALU.add).then_inc(biased.sem, 1)
                shift_agents(0, range(CHUNKS))
                shift_agents(1, range(DVE_SHIFTS, CHUNKS))

                def shift(c):
                    t2 = T2[0:SUB, c % 2, :].rearrange("p (m a) -> p m a", a=AGENTS)
                    pool.wait_ge(q_max.sem, q_max.at(i, c + 1))
                    pool.tensor_tensor(t2, t2, QM[0:SUB, c % 2, :].unsqueeze(2).broadcast_to([SUB, SUBS * HEADS, AGENTS]),
                                       ALU.subtract).then_inc(q_sub.sem, 1)

                def scale(c):
                    t2 = T2[0:SUB, c % 2, :].rearrange("p (m a) -> p m a", a=AGENTS)
                    pool.wait_ge(q_sum.sem, q_sum.at(i, c + 1))
                    pool.tensor_tensor(t2, t2, QS[0:SUB, c % 2, :].unsqueeze(2).broadcast_to([SUB, SUBS * HEADS, AGENTS]),
                                       ALU.mult).then_inc(q_mul.sem, 1)

                shift(0)
                scale(0)
                shift(1)
                for c in range(CHUNKS):
                    if c + 1 < CHUNKS:
                        scale(c + 1)
                    if c + 2 < CHUNKS:
                        shift(c + 2)
                    if prefetch and c in (3, 4):
                        norm_x(i, 1 + GN_X, c - 3)
                pool.wait_ge(gn_ab.sem, gn_ab.at(i, 1 + (GN_P if prefetch else GN_X)))
                carry(pool, i)
                for c in range(CHUNKS):
                    for t in range(HALVES):
                        p_out = KP[:, t, c * CHUNK:(c + 1) * CHUNK]
                        pool.tensor_scalar(p_out, p_out, AB[:, GN_P, 0, t:t + 1], AB[:, GN_P, 1, t:t + 1],
                                           ALU.mult, ALU.add).then_inc(p_affine.sem, 1)
                    pool.wait_ge(p_affine.sem, p_affine.at(i, 2 * (c + 1)))
                    pool.wait_ge(xr_loaded[c % 2].sem, xr_loaded[c % 2].at(i, c // 2 + 1))
                    kp = KP[:, :, c * CHUNK:(c + 1) * CHUNK]
                    pool.tensor_tensor(kp, kp, XR[:, c % 2, :, :], ALU.add).then_inc(res_done.sem, 1)

            if B > 1:
                with pool.Fori(0, B - 1) as i:
                    image(i, True)
            image(B - 1, False)

        @block.scalar
        def _(act):
            for s, credit in ((cv_free.sem, 2), (tr_free.sem, 2), (y_free.sem, 2)):
                act.sem_inc(s, credit)
            act.wait_ge(s_zero, ZEROED)
            for n in range(2 * TILES):
                c, s = n // SUBS, n % SUBS
                act.wait_ge(s_bmm, n + 1)
                if c >= 2 and s == 0:
                    act.wait_ge(s_table_out[c % 2], 16 * (c // 2))
                table = A[0:SUB, c % 2, 0:SUBS * ALL_AGENTS]
                if c < CHUNKS:
                    act.copy(table.rearrange("p (t s a) -> p s t a", t=HALVES, s=SUBS)[:, s, :, :],
                             SC[n % 2][0:SUB, 0:ALL_AGENTS].rearrange("p (t a) -> p t a", t=HALVES)).then_inc(s_bev, 1)
                else:
                    act.copy(table[:, s * ALL_AGENTS:(s + 1) * ALL_AGENTS], SC[n % 2][0:SUB, 0:ALL_AGENTS]).then_inc(
                        s_bev, 1)
            for s, n in tables_stored:
                act.wait_ge(s, n)

            def image(i, prefetch):
                def conv_out(first, dst):
                    for c in range(CHUNKS):
                        for t in range(HALVES):
                            n = first + 2 * c + t
                            if first == CV_K and t == 0:
                                act.wait_ge(stored[c].sem, stored[c].at(i, 0))
                            act.wait_ge(cv_full.sem, cv_full.at(i, n + 1))
                            act.copy(dst[:, t, c * CHUNK:(c + 1) * CHUNK], CV[n % 2][:, 0:CHUNK]).then_inc(cv_free.sem, 1)

                def norm_v(t):
                    if t == 0:
                        act.wait_ge(gn_ab.sem, gn_ab.at(i, 1 + GN_V))
                    act.activation(V_IN[:, t, :], V_IN[:, t, :], ACT.Identity, bias=AB[:, GN_V, 1, t:t + 1],
                                   scale=AB[:, GN_V, 0, t:t + 1]).then_inc(v_norm.sem, 1)

                def v_turned(t, u):
                    if t and u == 0:
                        act.wait_ge(av_done.sem, av_done.at(i, 1))
                    n = TR_VT[t] + u
                    act.wait_ge(tr_full.sem, tr_full.at(i, n + 1))
                    act.copy(VT[0:SUB, SUBS * u:SUBS * (u + 1), :, 0:2 * HEAD_DIM], TR[n % 2][0:SUB, :].rearrange(
                        "p (u g c) -> p u g c", u=SUBS, g=2)).then_inc(tr_free.sem, 1)

                def agent_v_out(t):
                    act.wait_ge(av_done.sem, av_done.at(i, t + 1))
                    for p in (2 * t, 2 * t + 1):
                        act.copy(AVS[0:V_ROWS, p % 2, :], AV[p]).then_inc(avs.sem, 1)

                def agent_weights(t, c):
                    if t and c >= DVE_SHIFTS:
                        act.wait_ge(shifted[2].sem, shifted[2].at(i, c - DVE_SHIFTS + 1))
                    else:
                        act.wait_ge(shifted[t].sem, shifted[t].at(i, c + 1))
                    scores = A_IN[:, t, SUBS * c:SUBS * (c + 1), :]
                    act.activation(scores, scores, ACT.Exp).then_inc(exp1.sem, 1)

                conv_out(CV_Q, Q)
                conv_out(CV_K, KP)
                conv_out(CV_V, V_IN)

                def query_weights(c):
                    act.wait_ge(q_sub.sem, q_sub.at(i, c + 1))
                    act.activation(T2[0:SUB, c % 2, :], T2[0:SUB, c % 2, :], ACT.Exp).then_inc(q_exp.sem, 1)

                for n in range(2 * CHUNKS):
                    act.wait_ge(sc_full.sem, sc_full.at(i, n + 1))
                    act.copy(A[0:SUB, 0, n * BANK:(n + 1) * BANK], SC[n % 2][0:SUB, 0:BANK]).then_inc(sc_free.sem, 1)
                norm_v(0)
                for u in range(CHUNKS):
                    v_turned(0, u)
                norm_v(1)
                for c in range(CHUNKS):
                    agent_weights(0, c)
                for c in range(CHUNKS):
                    agent_weights(1, c)
                agent_v_out(0)
                for u in range(CHUNKS):
                    v_turned(1, u)
                query_weights(0)
                agent_v_out(1)

                def projection_out(c):
                    for t in range(HALVES):
                        n = CV_P + 2 * c + t
                        act.wait_ge(cv_full.sem, cv_full.at(i, n + 1))
                        act.copy(KP[:, t, c * CHUNK:(c + 1) * CHUNK], CV[n % 2][:, 0:CHUNK]).then_inc(cv_free.sem, 1)

                for c in range(CHUNKS):
                    if c + 1 < CHUNKS:
                        query_weights(c + 1)
                    if c >= 2:
                        act.wait_ge(y_full.sem, y_full.at(i, 2 * (c - 1)))
                    for p in range(PAIRS):
                        n = TR_P2 + PAIRS * c + p
                        act.wait_ge(tr_full.sem, tr_full.at(i, n + 1))
                        act.copy(P2[0:PAIR, c % 2, p, :], TR[n % 2][0:PAIR, 0:CHUNK]).then_inc(tr_free.sem, 1)
                    for t in range(HALVES):
                        act.wait_ge(y_full.sem, y_full.at(i, 2 * c + t + 1))
                        if t == 0 and c >= 2:
                            act.wait_ge(cv_full.sem, cv_full.at(i, CV_P + 2 * (c - 1)))
                        act.activation(Y[:, c % 2, t, :], YA[t][:, 0:CHUNK], ACT.Identity,
                                       bias=dwc_b[:, t:t + 1]).then_inc(y_free.sem, 1)
                    if c:
                        projection_out(c - 1)
                projection_out(CHUNKS - 1)

            if B > 1:
                with act.Fori(0, B - 1) as i:
                    image(i, True)
            image(B - 1, False)

        @block.vector
        def _(dve):
            for s, credit in ((sc_free.sem, 2), (res_done.sem, 1)):
                dve.sem_inc(s, credit)
            for z in (V[:, :, :], DW[:, :, :, :], M1[:, :, :], M2[:, :, :], AGV[:, :, :], VG[:, :, :, :], A[:, :, :]):
                dve.memset(z, 0.0).then_inc(s_zero, 1)
            for z in (VT[:, :, :, 2 * HEAD_DIM:], ONES[:, :]):
                dve.memset(z, 1.0).then_inc(s_zero, 1)
            dve.wait_ge(s_zero, ZEROED)
            dve.wait_ge(s_const, 16 * 6)
            for g in range(PATCHES):
                for dx in range(3):
                    last = dve.tensor_scalar(DW[0:96, g, dx, :], eye32[0:96, :], DWC[0:96, g * 3 + dx:g * 3 + dx + 1],
                                             None, ALU.mult)
            last.then_inc(s_dwb, 1)

            taken = [0]

            def chain(i, ins):
                taken[0] += 1
                ins.then_inc(step.sem, 1)
                dve.wait_ge(step.sem, step.at(i, taken[0]))
                carry(dve, i)

            def norm_coefs(i, which, k, before):
                channel_means(i, before, ST)
                group_means(i, k, GROUP_SUMS)
                scale_and_shift(i, which)

            def channel_means(i, before, stats):
                chain(i, before)
                for t in range(HALVES):
                    last = dve.bn_aggr(MV[:, t, :], stats[:, t, :, :].rearrange("p c s -> p (c s)"))
                chain(i, last)
                chain(i, dve.tensor_tensor(SQ[:, :], MV[:, :, 0], MV[:, :, 0], ALU.mult))
                dve.tensor_tensor(MV[:, :, 1], MV[:, :, 1], SQ[:, :], ALU.add).then_inc(gn_mv.sem, 1)

            def group_means(i, k, sums):
                dve.wait_ge(gn_mm.sem, gn_mm.at(i, k))
                carry(dve, i)
                chain(i, dve.tensor_copy(GS[:, :, :], sums.rearrange("p (t k) -> p t k", t=HALVES)))
                chain(i, dve.tensor_tensor(SQ[:, :], GS[:, :, 0], GS[:, :, 0], ALU.mult))
                dve.tensor_tensor(VAR[:, :], GS[:, :, 1], SQ[:, :], ALU.subtract).then_inc(gn_read.sem, 1)
                dve.wait_ge(gn_read.sem, gn_read.at(i, k))
                carry(dve, i)

            def scale_and_shift(i, which):
                chain(i, dve.tensor_scalar(VAR[:, :], VAR[:, :], 0.0, EPS, ALU.max, ALU.add))
                dve.tensor_scalar(MINUS_HALF[:, :], VAR[:, :], -0.5, None, ALU.mult)
                chain(i, dve.tensor_scalar(HALF_BITS[:, :], VAR[:, :].bitcast(mybir.dt.int32), 1, None,
                                           ALU.logical_shift_right))
                chain(i, dve.tensor_scalar(RS[:, :].bitcast(mybir.dt.int32), HALF_BITS[:, :], -1.0, RSQRT_GUESS,
                                           ALU.mult, ALU.add))
                for _ in range(NEWTON):
                    chain(i, dve.tensor_tensor(SQ[:, :], RS[:, :], RS[:, :], ALU.mult))
                    chain(i, dve.tensor_tensor(SQ[:, :], SQ[:, :], MINUS_HALF[:, :], ALU.mult))
                    chain(i, dve.scalar_tensor_tensor(out=RS[:, :], in0=SQ[:, :], scalar=1.5, in1=RS[:, :],
                                                      op0=ALU.add, op1=ALU.mult))
                if which == GN_X:
                    chain(i, dve.tensor_copy(AB[:, which, 0, :], RS[:, :]))
                else:
                    chain(i, dve.tensor_tensor(AB[:, which, 0, :], RS[:, :], gn_par[:, which, 0, :], ALU.mult))
                chain(i, dve.tensor_tensor(SQ[:, :], GS[:, :, 0], AB[:, which, 0, :], ALU.mult))
                if which == GN_X:
                    dve.tensor_scalar(AB[:, which, 1, :], SQ[:, :], -1.0, None, ALU.mult).then_inc(gn_ab.sem, 1)
                else:
                    dve.tensor_tensor(AB[:, which, 1, :], gn_par[:, which, 1, :], SQ[:, :], ALU.subtract).then_inc(
                        gn_ab.sem, 1)

            def x_stats(t, c):
                return dve.bn_stats(STX[:, t, c, :], X[:, t, c * CHUNK:(c + 1) * CHUNK])

            def conv_stats(i, first, src):
                for c in range(CHUNKS):
                    for t in range(HALVES):
                        dve.wait_ge(cv_free.sem, cv_free.at(i, first + 2 * c + t + 1))
                        last = dve.bn_stats(ST[:, t, c, :], src[:, t, c * CHUNK:(c + 1) * CHUNK])
                return last

            dve.wait_ge(x_loaded.sem, x_loaded.at(0, CHUNKS))
            for c in range(CHUNKS):
                for t in range(HALVES):
                    last = x_stats(t, c)
            channel_means(0, last, STX)
            group_means(0, 0, GROUP_SUMS)
            scale_and_shift(0, GN_X)
            first_steps = taken[0]

            def image(i, prefetch):
                taken[0] = first_steps
                norm_coefs(i, GN_Q, 1 + GN_Q, conv_stats(i, CV_Q, Q))
                dve.wait_ge(gn_ab.sem, gn_ab.at(i, 1 + GN_Q))
                for t in range(HALVES):
                    last = dve.tensor_scalar(Q[:, t, :], Q[:, t, :], AB[:, GN_Q, 0, t:t + 1], AB[:, GN_Q, 1, t:t + 1],
                                             ALU.mult, ALU.add)
                chain(i, last)
                for t in range(HALVES):
                    last = dve.tensor_reduce(
                        AG[:, t, :].rearrange("p (y x) -> p y x", x=GRID),
                        Q[:, t, :].rearrange("p (y r x s) -> p y x r s", y=GRID, r=CELL, x=GRID), AX.XY, ALU.add)
                chain(i, last)
                for h in range(HALF_HEADS):
                    rows = slice(HEAD_DIM * h, HEAD_DIM * (h + 1))
                    last = dve.tensor_scalar(M2[rows, :, AGENTS * h:AGENTS * (h + 1)], AG[rows, :, :],
                                             SCALE / CELL ** 2, None, ALU.mult)
                last.then_inc(m2_ready.sem, 1)

                norm_coefs(i, GN_K, 1 + GN_K, conv_stats(i, CV_K, KP))
                dve.wait_ge(gn_ab.sem, gn_ab.at(i, 1 + GN_K))
                for t in range(HALVES):
                    last = dve.tensor_scalar(M1[:, t, :], M2[:, t, :], AB[:, GN_K, 0, t:t + 1], None, ALU.mult)
                last.then_inc(m1_ready.sem, 1)

                def add_agent_bias(n):
                    t, c, j = 1, n // 2 % CHUNKS, n % 2
                    dve.wait_ge(sc_full.sem, sc_full.at(i, n + 1))
                    if j == 0:
                        b = n // 2
                        dve.wait_ge(b1_loaded[b % 4].sem, b1_loaded[b % 4].at(i, b // 4 + 1))
                    dve.tensor_tensor(A[0:SUB, t, c * BLOCK + j * BANK:c * BLOCK + (j + 1) * BANK], SC[n % 2][0:SUB, 0:BANK],
                                      BIAS[0:SUB, n // 2 % 4, j * BANK:(j + 1) * BANK], ALU.add).then_inc(sc_free.sem, 1)

                def max_over_chunks(t, c):
                    if t == 0:
                        dve.wait_ge(biased.sem, biased.at(i, c + 1))
                    else:
                        dve.wait_ge(sc_free.sem, sc_free.at(i, 2 * (CHUNKS + c + 1)))
                    to = c // 2
                    last = dve.tensor_reduce(
                        CHUNK_MAX[0:SUB, to * HALF_AGENTS:(to + 1) * HALF_AGENTS],
                        A_IN[:, t, SUBS * (c - c % 2):SUBS * (c + 1), :].rearrange("p u a -> p a u"), AX.X, ALU.max)
                    if c == CHUNKS - 1:
                        chain(i, last)

                def max_over_tiles(t):
                    dve.tensor_reduce(TILE_MAX[0:SUB, :], CHUNK_MAX[0:SUB, :].rearrange("p (s a) -> p a s", s=SUBS),
                                      AX.X, ALU.max).then_inc(tile_max.sem, 1)

                def max_to_diagonal(t):
                    dve.wait_ge(max_turned.sem, max_turned.at(i, t + 1))
                    chain(i, dve.tensor_reduce(MAX[0:PAIR, :], MAX_TURNED.rearrange("p (g n) -> p g n", g=2), AX.X, ALU.max))
                    for g in range(2):
                        last = dve.tensor_scalar(MAX_DIAG[0:PAIR, g, :], ident[0:PAIR, 0:PAIR], MAX[0:PAIR, g:g + 1],
                                                 None, ALU.mult)
                    last.then_inc(max_diag.sem, 1)

                def max_to_row(t):
                    dve.wait_ge(max_spread.sem, max_spread.at(i, t + 1))
                    dve.tensor_copy(MAX_ROW[0:SUB, t, :], MAX_SPREAD).then_inc(max_row.sem, 1)

                def agent_values(p):
                    dve.wait_ge(avt.sem, avt.at(i, p + 1))
                    chain(i, dve.reciprocal(INV[0:PAIR, p:p + 1], AV_TURNED[p][:, 2 * HEAD_DIM:]))
                    dve.scalar_tensor_tensor(out=AGV[0:PAIR, p, :], in0=AV_TURNED[p][:, 0:2 * HEAD_DIM],
                                             scalar=INV[0:PAIR, p:p + 1], in1=pair_mask[0:PAIR, :],
                                             op0=ALU.mult, op1=ALU.mult).then_inc(agv.sem, 1)

                def query_scores(c):
                    for s in range(SUBS):
                        n = 2 * BLOCKS + SUBS * c + s
                        dve.wait_ge(sc_full.sem, sc_full.at(i, n + 1))
                        if s == 0:
                            if c >= 2:
                                dve.wait_ge(tr_full.sem, tr_full.at(i, TR_P2 + PAIRS * (c - 1)))
                            dve.wait_ge(b2_loaded[c % 2].sem, b2_loaded[c % 2].at(i, c // 2 + 1))
                        m = slice(s * ALL_AGENTS, (s + 1) * ALL_AGENTS)
                        last = dve.tensor_tensor(T2[0:SUB, c % 2, m], SC[n % 2][0:SUB, 0:ALL_AGENTS],
                                                 query_slots(c)[:, m], ALU.add)
                        last.then_inc(sc_free.sem, 1)
                    dve.wait_ge(sc_free.sem, sc_free.at(i, 2 * BLOCKS + SUBS * (c + 1)))
                    dve.tensor_reduce(QM[0:SUB, c % 2, :], T2[0:SUB, c % 2, :].rearrange("p (m a) -> p m a", a=AGENTS),
                                      AX.X, ALU.max).then_inc(q_max.sem, 1)

                def query_sums(c):
                    dve.wait_ge(q_exp.sem, q_exp.at(i, c + 1))
                    chain(i, dve.tensor_reduce(QS[0:SUB, c % 2, :],
                                               T2[0:SUB, c % 2, :].rearrange("p (m a) -> p m a", a=AGENTS),
                                               AX.X, ALU.add))
                    dve.reciprocal(QS[0:SUB, c % 2, :], QS[0:SUB, c % 2, :]).then_inc(q_sum.sem, 1)

                norm_coefs(i, GN_V, 1 + GN_V, conv_stats(i, CV_V, V_IN))
                for c in (1, 3):
                    max_over_chunks(0, c)
                dve.wait_ge(sc_free.sem, sc_free.at(i, 2 * CHUNKS))
                for c in range(CHUNKS):
                    add_agent_bias(2 * (CHUNKS + c))
                    add_agent_bias(2 * (CHUNKS + c) + 1)
                    if c == 0:
                        max_over_chunks(0, CHUNKS - 2)
                        max_over_chunks(0, CHUNKS - 1)
                        max_over_tiles(0)
                    if c == 1:
                        max_to_diagonal(0)
                    if c == 2:
                        max_to_row(0)
                    if c % 2 or c == CHUNKS - 1:
                        max_over_chunks(1, c)
                max_over_tiles(1)
                max_to_diagonal(1)
                max_to_row(1)
                dve.wait_ge(max_row.sem, max_row.at(i, 2))
                for c in range(DVE_SHIFTS):
                    scores = A_IN[:, 1, SUBS * c:SUBS * (c + 1), :]
                    dve.tensor_tensor(scores, scores, MAX_ROW[0:SUB, 1:2, :].broadcast_to([SUB, SUBS, HALF_AGENTS]),
                                      ALU.subtract).then_inc(shifted[1].sem, 1)
                dve.wait_ge(av_done.sem, av_done.at(i, 1))
                query_scores(0)
                query_sums(0)
                agent_values(0)
                agent_values(1)
                query_scores(1)
                agent_values(2)
                agent_values(3)
                for c in range(CHUNKS):
                    if c + 1 < CHUNKS:
                        query_sums(c + 1)
                    if prefetch and c == HALVES + 1:
                        group_means(i, 1 + GN_X, GROUP_SUMS_X)
                    if c + 2 < CHUNKS:
                        query_scores(c + 2)
                    if c:
                        for t in range(HALVES):
                            dve.wait_ge(cv_free.sem, cv_free.at(i, CV_P + 2 * (c - 1) + t + 1))
                            dve.bn_stats(ST[:, t, c - 1, :], KP[:, t, (c - 1) * CHUNK:c * CHUNK])
                    if prefetch and c < HALVES:
                        if c == 0:
                            dve.wait_ge(x_loaded.sem, x_loaded.at(i + 1, CHUNKS))
                        for x_chunk in range(CHUNKS - 1 if c else CHUNKS):
                            x_stats(c, x_chunk)
                    if prefetch and c == HALVES:
                        channel_means(i, x_stats(1, CHUNKS - 1), STX)
                    if prefetch and c == HALVES + 1:
                        scale_and_shift(i, GN_X)
                for t in range(HALVES):
                    dve.wait_ge(cv_free.sem, cv_free.at(i, CV_P + 2 * (CHUNKS - 1) + t + 1))
                    last = dve.bn_stats(ST[:, t, CHUNKS - 1, :], KP[:, t, (CHUNKS - 1) * CHUNK:])
                norm_coefs(i, GN_P, 1 + (GN_P if prefetch else GN_X), last)
                if prefetch:
                    assert taken[0] - first_steps == STEPS, taken[0] - first_steps

            if B > 1:
                with dve.Fori(0, B - 1) as i:
                    image(i, True)
            image(B - 1, False)

        @block.tensor
        def _(pe):
            pe.sem_inc(dw_done.sem, 2)
            pe.wait_ge(s_const, 16 * 6)
            for n in range(2 * TILES):
                if n >= 2:
                    pe.wait_ge(s_bev, n - 1)
                table, u = n // TILES, n % TILES
                at = ALL_AGENTS * (2 * (u * (SUB // W) // WINDOW) + table)
                pe.matmul(SC[n % 2][0:SUB, 0:ALL_AGENTS], Q[0:BASIS, 0, SUB * u:SUB * (u + 1)],
                          KP[0:BASIS, 0, at:at + ALL_AGENTS], start=True, stop=True).then_inc(s_bmm, 1)

            def group_stats(i, k, sums=GROUP_SUMS):
                pe.wait_ge(gn_mv.sem, gn_mv.at(i, k))
                pe.matmul(sums, group_mean, MV[:, :, :].rearrange("p t k -> p (t k)"), start=True, stop=True).then_inc(
                    gn_mm.sem, 1)

            pe.wait_ge(s_dwb, 1)
            group_stats(0, 0)

            def conv(i, first, j, c, rhs):
                for t in range(HALVES):
                    n = first + 2 * c + t
                    pe.wait_ge(cv_free.sem, cv_free.at(i, n + 1 - 2))
                    for k in range(HALVES):
                        last = pe.matmul(CV[n % 2][:, 0:CHUNK], WT[:, j, k, t * P:(t + 1) * P], rhs(c, k),
                                         start=(k == 0), stop=(k == HALVES - 1))
                    last.then_inc(cv_full.sem, 1)

            def x_in(c, k):
                return X[:, k, c * CHUNK:(c + 1) * CHUNK]

            def first_convs(i):
                pe.wait_ge(x_norm.sem, x_norm.at(i, HALVES))
                for c in range(2):
                    conv(i, CV_Q, 0, c, x_in)

            first_convs(0)

            def image(i, prefetch):
                for c in range(2, CHUNKS):
                    conv(i, CV_Q, 0, c, x_in)
                for c in range(CHUNKS):
                    conv(i, CV_K, 1, c, x_in)
                    if c == 1:
                        group_stats(i, 1 + GN_Q)
                for c in range(CHUNKS):
                    conv(i, CV_V, 2, c, x_in)
                    if c == 2:
                        group_stats(i, 1 + GN_K)

                def turn_v(t):
                    pe.wait_ge(v_norm.sem, v_norm.at(i, t + 1))
                    for u in range(CHUNKS):
                        n = TR_VT[t] + u
                        pe.wait_ge(tr_free.sem, tr_free.at(i, n + 1 - 2))
                        for s in range(SUBS):
                            v = V_IN[:, t, SUB * (SUBS * u + s):SUB * (SUBS * u + s + 1)]
                            last = pe.transpose(TR[n % 2][0:SUB, s * P:(s + 1) * P], v, ident)
                        last.then_inc(tr_full.sem, 1)

                def agent_scores(n):
                    t, u = n // (2 * CHUNKS), 2 * (n % (2 * CHUNKS))
                    pe.wait_ge(sc_free.sem, sc_free.at(i, n + 1 - 2))
                    for j in range(2):
                        last = pe.matmul(SC[n % 2][0:SUB, j * HALF_AGENTS:(j + 1) * HALF_AGENTS],
                                         KP[:, t, SUB * (u + j):SUB * (u + j + 1)], M1[:, t, :], start=True, stop=True)
                    last.then_inc(sc_full.sem, 1)

                def turn_agent_v(p):
                    pe.wait_ge(avs.sem, avs.at(i, p + 1))
                    pe.transpose(AV_TURNED[p], AVS[0:V_ROWS, p % 2, :], ident[0:V_ROWS, 0:V_ROWS]).then_inc(avt.sem, 1)

                def turn_maxima(t):
                    pe.wait_ge(tile_max.sem, tile_max.at(i, t + 1))
                    for g in range(2):
                        last = pe.transpose(MAX_TURNED[:, SUB * g:SUB * (g + 1)], TILE_MAX[0:SUB, PAIR * g:PAIR * (g + 1)],
                                            ident[0:SUB, 0:SUB])
                    last.then_inc(max_turned.sem, 1)

                def spread_maxima(t):
                    pe.wait_ge(max_diag.sem, max_diag.at(i, t + 1))
                    pe.matmul(MAX_SPREAD, ONES[0:PAIR, :], MAX_DIAG[0:PAIR, :, :].rearrange("p g a -> p (g a)"),
                              start=True, stop=True).then_inc(max_spread.sem, 1)

                def agent_sums(t, chunks=range(CHUNKS)):
                    if t == 0 and chunks[0] == 0:
                        pe.wait_ge(gn_read.sem, gn_read.at(i, 1 + GN_V))
                    pe.wait_ge(tr_free.sem, tr_free.at(i, TR_VT[t] + CHUNKS))
                    for c in chunks:
                        pe.wait_ge(exp1.sem, exp1.at(i, CHUNKS * t + c + 1))
                        for u in range(SUBS * c, SUBS * (c + 1)):
                            for g in range(2):
                                last = pe.matmul(AV[2 * t + g], VT[0:SUB, u, g, :],
                                                 A_IN[:, t, u, PAIR * g:PAIR * (g + 1)],
                                                 start=(u == 0), stop=(u == TILES - 1))
                    if chunks[-1] == CHUNKS - 1:
                        last.then_inc(av_done.sem, 1)

                def query_scores(c, tiles=range(SUBS)):
                    for s in tiles:
                        u = SUBS * c + s
                        n = 2 * BLOCKS + u
                        pe.wait_ge(sc_free.sem, sc_free.at(i, n + 1 - 2))
                        for t in range(HALVES):
                            last = pe.matmul(SC[n % 2][0:SUB, HALF_AGENTS * t:HALF_AGENTS * (t + 1)],
                                             Q[:, t, SUB * u:SUB * (u + 1)], M2[:, t, :], start=True, stop=True)
                        last.then_inc(sc_full.sem, 1)

                pe.wait_ge(m1_ready.sem, m1_ready.at(i, 1))
                for n in range(2 * CHUNKS):
                    agent_scores(n)
                    if n == 1:
                        group_stats(i, 1 + GN_V)
                for n in range(2 * CHUNKS, 4 * CHUNKS):
                    agent_scores(n)
                    if n == 2 * CHUNKS + 3:
                        turn_v(0)
                        turn_maxima(0)
                    if n == 2 * CHUNKS + 5:
                        spread_maxima(0)
                    if n == 2 * CHUNKS + 11:
                        agent_sums(0, (0,))
                agent_sums(0, (1, 2))
                turn_maxima(1)
                agent_sums(0, (3,))
                spread_maxima(1)
                agent_sums(0, range(4, CHUNKS))
                query_scores(0)
                turn_v(1)
                turn_agent_v(0)
                turn_agent_v(1)
                agent_sums(1)
                query_scores(1)
                turn_agent_v(2)
                turn_agent_v(3)

                def depthwise(c, t):
                    if c == 0 and t == 0:
                        pe.wait_ge(agv.sem, agv.at(i, 2))
                    pe.wait_ge(vg_loaded.sem, vg_loaded.at(i, c + 1))
                    pe.wait_ge(y_free.sem, y_free.at(i, 2 * c + t + 1 - 2))
                    for dx, to, of in ((1, 0, 0), (0, 1, 0), (2, 0, 1)):
                        w = W if dx == 1 else W - 1
                        for q in range(4):
                            out = YA[t][32 * q:32 * (q + 1), 0:CHUNK].rearrange("p (h w) -> p h w", w=W)[:, :, to:to + w]
                            rows = VG[:, t, q, :].rearrange("p (h w) -> p h w", w=W)[:, :, of:of + w]
                            last = pe.matmul(out, DW[:, 4 * t + q, dx, :], rows, start=(dx == 1), stop=False,
                                             skip_group_check=True)
                    last.then_inc(dw_done.sem, 1)

                def turn_query(c, pairs):
                    pe.wait_ge(q_mul.sem, q_mul.at(i, c + 1))
                    for p in pairs:
                        n = TR_P2 + PAIRS * c + p
                        pe.wait_ge(tr_free.sem, tr_free.at(i, n + 1 - 2))
                        for s in range(SUBS):
                            m = s * ALL_AGENTS + PAIR * p
                            last = pe.transpose(TR[n % 2][0:PAIR, SUB * s:SUB * (s + 1)],
                                                T2[0:SUB, c % 2, m:m + PAIR], ident[0:SUB, 0:SUB])
                        last.then_inc(tr_full.sem, 1)

                def attend(c, t):
                    if c == 0:
                        pe.wait_ge(agv.sem, agv.at(i, PAIRS))
                    pe.wait_ge(tr_free.sem, tr_free.at(i, TR_P2 + PAIRS * c + 2 * t + 2))
                    for g in range(2):
                        last = pe.matmul(YA[t][64 * g:64 * (g + 1), 0:CHUNK], AGV[:, 2 * t + g, :],
                                         P2[:, c % 2, 2 * t + g, :], start=False, stop=True, skip_group_check=True)
                    last.then_inc(y_full.sem, 1)

                def project(c):
                    pe.wait_ge(y_free.sem, y_free.at(i, 2 * (c + 1)))
                    conv(i, CV_P, 3, c, lambda c, k: Y[:, c % 2, k, :])

                for c in range(CHUNKS):
                    depthwise(c, 0)
                    if prefetch and c == HALVES + 1:
                        pe.wait_ge(cv_free.sem, cv_free.at(i, CV_P + 2 * (c - 1)))
                        group_stats(i, 1 + GN_X, GROUP_SUMS_X)
                    depthwise(c, 1)
                    turn_query(c, (0, 1))
                    if c + 2 < CHUNKS:
                        query_scores(c + 2, (0, 1))
                    turn_query(c, (2, 3))
                    attend(c, 0)
                    if c + 2 < CHUNKS:
                        query_scores(c + 2, (2,))
                    attend(c, 1)
                    if c + 2 < CHUNKS:
                        query_scores(c + 2, (3,))
                    if prefetch and c == HALVES + 1:
                        pe.wait_ge(gn_read.sem, gn_read.at(i, 1 + GN_X))
                    if c:
                        project(c - 1)
                project(CHUNKS - 1)
                if prefetch:
                    first_convs(i + 1)
                group_stats(i, 1 + (GN_P if prefetch else GN_X))

            if B > 1:
                with pe.Fori(0, B - 1) as i:
                    image(i, True)
            image(B - 1, False)


TR_VT = [0, CHUNKS]
TR_P2 = 2 * CHUNKS
STEPS = 5 * (7 + 3 + 3 * NEWTON) + 2 + 2 * HALVES + PAIRS + CHUNKS
ZEROED = 9


def layouts(x, p):
    B = x.shape[0]
    at = lambda n: np.asarray(p[f"L0_conv_{n}"])
    by_half = lambda v: v.reshape(HALVES, P).T
    weights = np.stack([at(f"{n}_w").T.reshape(HALVES, P, C) for n in "qkvp"])
    params = [by_half(at(f"{n}_g{k}")) for n in "qkv" for k in "wb"]
    params += [np.zeros((P, 2 * HALVES), np.float32)]
    params += [by_half(at(f"p_g{k}")) for k in "wb"] + [by_half(at("dwc_b"))]
    taps = at("dwc_w").reshape(PATCHES, HEAD_DIM, 3, 3).transpose(2, 1, 0, 3)
    grids = [at(f"{n}_bias").reshape(ALL_AGENTS, GRID * GRID).T for n in ("an", "na")]
    columns = [at("aw_bias").reshape(ALL_AGENTS, W).T,
               at("wa_bias").reshape(HEADS, W, AGENTS).transpose(1, 0, 2).reshape(W, ALL_AGENTS)]
    rows = [at("ah_bias").reshape(ALL_AGENTS, H).T,
            at("ha_bias").reshape(HEADS, H, AGENTS).transpose(1, 0, 2).reshape(H, ALL_AGENTS)]
    rows = [np.concatenate([r, np.zeros((WINDOWS * WINDOW - H, ALL_AGENTS), r.dtype)]) for r in rows]
    coefs = np.concatenate([np.concatenate([grids[j], columns[j], rows[j][WINDOW * w:WINDOW * (w + 1)]])
                            for w in range(WINDOWS) for j in range(2)], axis=1)
    where = (np.arange(H) + 0.5) / CELL - 0.5
    line = np.maximum(0, 1 - np.abs(where[None, :] - np.arange(GRID)[:, None]))
    line /= line.sum(0)
    grid = np.einsum("iy,jx->ijyx", line, line).reshape(GRID * GRID, N)
    ys = np.repeat(np.tile(np.eye(WINDOW), (1, WINDOWS))[:, :H], W, axis=1)
    xs = np.tile(np.eye(W), (1, H))
    same_group = np.kron(np.eye(P // GROUP), np.ones((GROUP, GROUP))) / GROUP
    heads = np.zeros((P, 2 * HEAD_DIM))
    heads[:PAIR] = np.kron(np.eye(2), np.ones((AGENTS, HEAD_DIM)))
    constants = np.concatenate([np.eye(P), same_group, np.tile(np.eye(HEAD_DIM), (P // HEAD_DIM, 1)), heads], axis=1)
    return {
        "x": np.asarray(x).reshape(B, C, N),
        "weights": np.ascontiguousarray(weights.transpose(2, 0, 1, 3).reshape(P, 4 * HALVES * C)),
        "params": np.ascontiguousarray(np.concatenate(params, axis=1)),
        "taps": np.ascontiguousarray(taps.reshape(3 * HEAD_DIM, PATCHES * 3)),
        "bias_coefs": np.ascontiguousarray(coefs),
        "basis": np.concatenate([grid, xs, ys]).astype(np.float32),
        "constants": constants.astype(np.float32),
    }


def kernel(x, **params):
    import concourse.bacc as bacc
    from concourse.bass_utils import run_bass_kernel_spmd

    B = x.shape[0]
    arrays = layouts(x, params)
    nc = bacc.Bacc("TRN2", target_bir_lowering=False, num_devices=1)
    dram = {n: nc.dram_tensor(n, v.shape, F32, kind="ExternalInput").ap() for n, v in arrays.items()}
    dram["out"] = nc.dram_tensor("out", (B, C, N), F32, kind="ExternalOutput").ap()
    attention_block(nc, B, dram)
    r = run_bass_kernel_spmd(nc, [arrays], core_ids=[0])
    return r.results[0]["out"].reshape(B, C, H, W)
```
